# Optimizing a Trainium2 kernel written in Bass

```python
import numpy as np
import jax
import jax.numpy as jnp

def _softmax(x, axis=-1):
    return jax.nn.softmax(x, axis=axis)

def _gelu(x):
    return jax.nn.gelu(x, approximate=True)

def _silu(x):
    return jax.nn.silu(x)

def _sigmoid(x):
    return jax.nn.sigmoid(x)

def _layernorm(x, axis=-1, eps=1e-05):
    m = jnp.mean(x, axis=axis, keepdims=True)
    v = jnp.var(x, axis=axis, keepdims=True)
    return (x - m) / jnp.sqrt(v + eps)

def _scatter_add(tgt, idx, src, axis=0):
    return tgt.at[idx].add(src)

def _segment_sum(src, seg, n):
    return jax.ops.segment_sum(src, seg, n)
kernel_name = 'mk_adaln_d1_jaxref_r8_7a103b'

def setup_inputs(seed: int=0):
    np.random.seed(seed)
    _w = jnp.asarray

    def _L0_attn_setup():
        import jax, jax.numpy as jnp
        import numpy as np
        HIDDEN = 256
        KEY = 256
        EPS = 1e-05
        key = jax.random.key(seed)
        k1, k2, k3 = jax.random.split(key, 3)
        B, S = (4, 256)
        x = jax.random.normal(k1, (B, S, HIDDEN), dtype=jnp.float32)
        bq = 1.0 / np.sqrt(HIDDEN)
        qkv = jax.random.uniform(k2, (HIDDEN, KEY * 3), minval=-bq, maxval=bq, dtype=jnp.float32)
        bo = 1.0 / np.sqrt(KEY)
        o_proj = jax.random.uniform(k3, (KEY, HIDDEN), minval=-bo, maxval=bo, dtype=jnp.float32)
        gamma = jnp.ones((HIDDEN,), dtype=jnp.float32)
        beta = jnp.zeros((HIDDEN,), dtype=jnp.float32)
        return {'x': x, 'qkv': qkv, 'o_proj': o_proj, 'gamma': gamma, 'beta': beta}
    _L0_attn_in = _L0_attn_setup()

    def _L0_ffn_setup():
        import jax, jax.numpy as jnp
        import numpy as np
        E = 32
        K = 4
        G = 4
        TG = 2
        H = 256
        F = 128
        FS = 256
        SCALE = 2.0
        B, S = (2, 128)
        N = B * S
        CAP = 2 * (N * K // E)

        def _gate(x, gate_w, gate_bias):
            logits = x @ gate_w.T
            scores = jax.nn.sigmoid(logits)
            sc = scores + gate_bias
            n = x.shape[0]
            grp = sc.reshape(n, G, E // G)
            group_scores = jax.lax.top_k(grp, 2)[0].sum(-1)
            _, gidx = jax.lax.top_k(group_scores, TG)
            gmask = jnp.zeros((n, G), sc.dtype).at[jnp.arange(n)[:, None], gidx].set(1.0)
            smask = jnp.repeat(gmask, E // G, axis=1)
            tmp = jnp.where(smask > 0, sc, 0.0)
            _, topk_idx = jax.lax.top_k(tmp, K)
            topk_w = jnp.take_along_axis(scores, topk_idx, axis=1)
            topk_w = topk_w / (topk_w.sum(-1, keepdims=True) + 1e-20)
            return (topk_idx, topk_w * SCALE)

        def _moe(x, topk_idx, topk_w, w1, w2, w3):
            n = x.shape[0]
            flat_e = topk_idx.reshape(-1)
            oh = jax.nn.one_hot(flat_e, E, dtype=jnp.int32)
            pos = (jnp.cumsum(oh, axis=0) * oh).sum(-1) - 1
            keep = pos < CAP
            slot = jnp.where(keep, pos, CAP)
            x_rep = jnp.repeat(x, K, axis=0)
            buf = jnp.zeros((E, CAP, H), x.dtype).at[flat_e, slot].set(x_rep, mode='drop')
            h = jax.nn.silu(jnp.einsum('ech,ehf->ecf', buf, w1)) * jnp.einsum('ech,ehf->ecf', buf, w3)
            ob = jnp.einsum('ecf,efh->ech', h, w2)
            y = ob[flat_e, jnp.minimum(slot, CAP - 1)]
            y = jnp.where(keep[:, None], y, 0.0)
            return (y.reshape(n, K, H) * topk_w[:, :, None]).sum(1)
        key = jax.random.key(seed)
        ks = jax.random.split(key, 9)
        w = 0.02
        return {'hidden_states': jax.random.normal(ks[0], (B, S, H), jnp.float32), 'gate_w': jax.random.normal(ks[1], (E, H), jnp.float32) * w, 'gate_bias': jax.random.normal(ks[2], (E,), jnp.float32) * w, 'w1': jax.random.normal(ks[3], (E, H, F), jnp.float32) * w, 'w2': jax.random.normal(ks[4], (E, F, H), jnp.float32) * w, 'w3': jax.random.normal(ks[5], (E, H, F), jnp.float32) * w, 'shared_gate': jax.random.normal(ks[6], (H, FS), jnp.float32) * w, 'shared_up': jax.random.normal(ks[7], (H, FS), jnp.float32) * w, 'shared_down': jax.random.normal(ks[8], (FS, H), jnp.float32) * w}
    _L0_ffn_in = _L0_ffn_setup()
    _L0_c = _w((lambda *s: np.random.randn(*s).astype(np.float32) * 0.05)(1, 256))
    _L0_wmod = _w((lambda *s: np.random.randn(*s).astype(np.float32) * 0.05)(256, 6 * 256) * 256 ** (-0.5))
    _d = {'L0_attn_x': _L0_attn_in['x'], 'L0_attn_qkv': _L0_attn_in['qkv'], 'L0_attn_o_proj': _L0_attn_in['o_proj'], 'L0_attn_gamma': _L0_attn_in['gamma'], 'L0_attn_beta': _L0_attn_in['beta'], 'L0_ffn_gate_w': _L0_ffn_in['gate_w'], 'L0_ffn_gate_bias': _L0_ffn_in['gate_bias'], 'L0_ffn_w1': _L0_ffn_in['w1'], 'L0_ffn_w2': _L0_ffn_in['w2'], 'L0_ffn_w3': _L0_ffn_in['w3'], 'L0_ffn_shared_gate': _L0_ffn_in['shared_gate'], 'L0_ffn_shared_up': _L0_ffn_in['shared_up'], 'L0_ffn_shared_down': _L0_ffn_in['shared_down'], 'L0_c': _L0_c, 'L0_wmod': _L0_wmod}
    _x0 = _d['L0_attn_x']
    _d['L0_attn_x'] = jax.random.normal(jax.random.fold_in(jax.random.key(seed), 1), (1, 1024, 256), dtype=_x0.dtype)
    del _x0
    return _d

def reference(L0_attn_x, L0_attn_qkv, L0_attn_o_proj, L0_attn_gamma, L0_attn_beta, L0_ffn_gate_w, L0_ffn_gate_bias, L0_ffn_w1, L0_ffn_w2, L0_ffn_w3, L0_ffn_shared_gate, L0_ffn_shared_up, L0_ffn_shared_down, L0_c, L0_wmod):

    def _L0_attn_ref(x, qkv, o_proj, gamma, beta):
        import jax, jax.numpy as jnp
        import numpy as np
        HIDDEN = 256
        KEY = 256
        EPS = 1e-05
        residual = x
        mu = jnp.mean(x, axis=-1, keepdims=True)
        var = jnp.mean((x - mu) ** 2, axis=-1, keepdims=True)
        x_norm = (x - mu) / jnp.sqrt(var + EPS) * gamma + beta
        q = x_norm @ qkv[:, :KEY]
        k = x_norm @ qkv[:, KEY:2 * KEY]
        v = x_norm @ qkv[:, 2 * KEY:]
        scale = 1.0 / jnp.sqrt(jnp.float32(KEY))
        scores = jnp.einsum('bsk,btk->bst', q, k) * scale
        S_len = x.shape[1]
        causal = jnp.tril(jnp.ones((S_len, S_len), dtype=bool))
        scores = jnp.where(causal[None], scores, -jnp.inf)
        attn = jax.nn.softmax(scores, axis=-1)
        out = attn @ v
        out = out @ o_proj
        return out + residual

    def _L0_ffn_ref(hidden_states, gate_w, gate_bias, w1, w2, w3, shared_gate, shared_up, shared_down):
        import jax, jax.numpy as jnp
        import numpy as np
        E = 32
        K = 4
        G = 4
        TG = 2
        H = 256
        F = 128
        FS = 256
        SCALE = 2.0
        B, S = (2, 128)
        N = B * S
        CAP = 2 * (N * K // E)

        def _gate(x, gate_w, gate_bias):
            logits = x @ gate_w.T
            scores = jax.nn.sigmoid(logits)
            sc = scores + gate_bias
            n = x.shape[0]
            grp = sc.reshape(n, G, E // G)
            group_scores = jax.lax.top_k(grp, 2)[0].sum(-1)
            _, gidx = jax.lax.top_k(group_scores, TG)
            gmask = jnp.zeros((n, G), sc.dtype).at[jnp.arange(n)[:, None], gidx].set(1.0)
            smask = jnp.repeat(gmask, E // G, axis=1)
            tmp = jnp.where(smask > 0, sc, 0.0)
            _, topk_idx = jax.lax.top_k(tmp, K)
            topk_w = jnp.take_along_axis(scores, topk_idx, axis=1)
            topk_w = topk_w / (topk_w.sum(-1, keepdims=True) + 1e-20)
            return (topk_idx, topk_w * SCALE)

        def _moe(x, topk_idx, topk_w, w1, w2, w3):
            n = x.shape[0]
            flat_e = topk_idx.reshape(-1)
            oh = jax.nn.one_hot(flat_e, E, dtype=jnp.int32)
            pos = (jnp.cumsum(oh, axis=0) * oh).sum(-1) - 1
            keep = pos < CAP
            slot = jnp.where(keep, pos, CAP)
            x_rep = jnp.repeat(x, K, axis=0)
            buf = jnp.zeros((E, CAP, H), x.dtype).at[flat_e, slot].set(x_rep, mode='drop')
            h = jax.nn.silu(jnp.einsum('ech,ehf->ecf', buf, w1)) * jnp.einsum('ech,ehf->ecf', buf, w3)
            ob = jnp.einsum('ecf,efh->ech', h, w2)
            y = ob[flat_e, jnp.minimum(slot, CAP - 1)]
            y = jnp.where(keep[:, None], y, 0.0)
            return (y.reshape(n, K, H) * topk_w[:, :, None]).sum(1)
        b, s, h = hidden_states.shape
        x = hidden_states.reshape(-1, h)
        topk_idx, topk_w = _gate(x, gate_w, gate_bias)
        out = _moe(x, topk_idx, topk_w, w1, w2, w3)
        shared = jax.nn.silu(x @ shared_gate) * (x @ shared_up) @ shared_down
        return (out + shared).reshape(b, s, h)
    x = L0_attn_x
    mod = (_silu(L0_c) @ L0_wmod).reshape(L0_c.shape[0], 6, 1, -1)
    sa, ca, ga, sb, cb, gb = (mod[:, 0], mod[:, 1], mod[:, 2], mod[:, 3], mod[:, 4], mod[:, 5])
    ga = (2 * (ga >= 0) - 1) * jnp.maximum(jnp.abs(ga), 0.25)
    gb = (2 * (gb >= 0) - 1) * jnp.maximum(jnp.abs(gb), 0.25)
    h = _layernorm(x, axis=-1) * (1 + ca) + sa
    x = x + ga * _L0_attn_ref(h, L0_attn_qkv, L0_attn_o_proj, L0_attn_gamma, L0_attn_beta)
    h = _layernorm(x, axis=-1) * (1 + cb) + sb
    x = x + gb * _L0_ffn_ref(h, L0_ffn_gate_w, L0_ffn_gate_bias, L0_ffn_w1, L0_ffn_w2, L0_ffn_w3, L0_ffn_shared_gate, L0_ffn_shared_up, L0_ffn_shared_down)
    return x

_drawn_inputs = setup_inputs


def setup_inputs(seed=0):
    import zlib

    import numpy as np

    out = dict(_drawn_inputs(seed))
    spreads = {'L0_attn_gamma': (1.0, 0.6), 'L0_attn_beta': (0.0, 0.8)}
    factors = {'L0_attn_qkv': 5.357,
     'L0_attn_o_proj': 5.547,
     'L0_ffn_gate_w': 8.0,
     'L0_ffn_gate_bias': 8.0,
     'L0_ffn_w1': 8.0,
     'L0_ffn_w2': 8.0,
     'L0_ffn_w3': 8.0,
     'L0_ffn_shared_gate': 8.0,
     'L0_ffn_shared_up': 8.0,
     'L0_ffn_shared_down': 8.0}
    for name, (base, spread) in spreads.items():
        noise = np.random.default_rng([zlib.crc32(name.encode()), seed]).standard_normal(out[name].shape)
        drawn = base * np.exp(spread * noise) if base else spread * noise
        out[name] = jnp.asarray(drawn.astype(out[name].dtype))
    for name, factor in factors.items():
        out[name] = (out[name] * factor).astype(out[name].dtype)
    return out
```

```python
from contextlib import ExitStack

import concourse.bass as bass
from concourse import mybir

P = 128
ALU = mybir.AluOpType
ACT = mybir.ActivationFunctionType
AX_X = mybir.AxisListType.X
F32 = mybir.dt.float32
BF16 = mybir.dt.bfloat16
I32 = mybir.dt.int32
U32 = mybir.dt.uint32

LN_EPS = 1e-5
TOPK = 4
GROUPS = 4
TOP_GROUPS = 2
ROUTED_SCALE = 2.0
CAP = 2 * (2 * 128 * TOPK // 32)
MASKED = -1e30
SKIP = 8192.0


def adaln_attention_moe(nc, x, qkv, o_proj, gamma, beta, gate_w, gate_bias, w1, w2, w3,
                        shared_gate, shared_up, shared_down, c, wmod, out):
    _, N, H = x.shape
    E, _, F = w1.shape
    FS = shared_gate.shape[1]
    KT = H // P
    NT = N // P
    NB = NT // 2
    EG = E // GROUPS
    PAIRS = E // 2
    CHUNKS = PAIRS // 4
    EGROUPS = PAIRS // 2
    ROW = H + 2 * TOPK
    SCALE = float(H) ** -0.5
    assert (H, F, FS, CAP, KT, NT, E) == (256, 128, 256, 64, 2, 8, 32)

    x_d = x.rearrange("b (i p) h -> p (b i) h", p=P)
    out_d = out.rearrange("b (i p) h -> p (b i) h", p=P)
    col = lambda v: v.rearrange("(p k) -> p k", k=KT)
    row_bcast = lambda v: v.rearrange("(a n) -> a n", a=1).to_broadcast([P, v.shape[0]])
    slots_d = nc.dram_tensor("slots", (E * CAP, ROW), F32).ap()
    results_d = nc.dram_tensor("results", (N * TOPK, H), F32).ap()
    slots_rows = slots_d.rearrange("(r p) c -> p r c", p=P)
    results_rows = results_d.rearrange("(i p k) h -> p i (k h)", p=P, k=TOPK)

    with ExitStack() as ctx:
        sb = lambda name, shape, dt=F32: ctx.enter_context(nc.sbuf_tensor(name, shape, dt))
        sem = lambda name: ctx.enter_context(nc.semaphore(name))
        bank = [ctx.enter_context(nc.psum_tensor(f"bank{i}", [P, 512], F32)) for i in range(8)]

        w1_sb = sb("w1_sb", [P, E, KT, F])
        w3_sb = sb("w3_sb", [P, E, KT, F])
        w2_sb = sb("w2_sb", [P, E, H])
        shg_sb = sb("shg_sb", [P, KT, FS])
        shu_sb = sb("shu_sb", [P, KT, FS])
        shd_sb = sb("shd_sb", [P, FS // P, H])
        bias_b = sb("bias_b", [P, E])
        gatew_sb = sb("gatew_sb", [E, H])
        gateT = sb("gateT", [P, KT, E])
        gb_col = sb("gb_col", [P, 2, KT])
        ident = sb("ident", [P, P])
        ident_bf = sb("ident_bf", [P, P], BF16)
        causal_bf = sb("causal_bf", [P, P], BF16)
        earlier_bf = sb("earlier_bf", [P, P], BF16)
        ones_bf = sb("ones_bf", [P, P], BF16)
        ones_f = sb("ones_f", [P, P])
        iota_i = sb("iota_i", [P, 128], I32)
        enum = sb("enum", [P, E])
        slot_expert = sb("slot_expert", [P, PAIRS])
        lower = sb("lower", [P, GROUPS, GROUPS])

        base = sb("base", [P, NT, H])
        rows = sb("rows", [P, NT, ROW])
        h2T = sb("h2T", [P, KT, N])
        aT = sb("aT", [P, FS // P, N])
        mod = sb("mod", [P, 6, H])
        modc = sb("modc", [P, 2, KT])

        last_q = slice(3 * E // 4, E)
        flat = lambda t, k: t.rearrange("p e k f -> p (e k f)") if k else t.rearrange("p e n -> p (e n)")
        place1, place3, place2 = flat(w1_sb[:, last_q], 1), flat(w3_sb[:, last_q], 1), flat(w2_sb[:, last_q], 0)
        wmod_a = place3[:, 0:1024].rearrange("p (k n) -> p k n", k=KT)
        wmod_b = place1.rearrange("p (k n) -> p k n", k=KT)
        wo_sb = place3[:, 1024:1536].rearrange("p (k n) -> p k n", k=KT)
        hn = place3[:, 1536:2048].rearrange("p (i n) -> p i n", i=2)
        qkv_sb = place2[:, 0:1536].rearrange("p (k n) -> p k n", k=KT)
        wqk = place2[:, 1536:2048].rearrange("p (k n) -> p k n", k=KT)

        ARENA = 10368
        arena = sb("arena", [P, ARENA])
        at = 0

        def take(n):
            nonlocal at
            at += n
            assert at <= ARENA
            return arena[:, at - n:at]

        wT = take(3 * KT * KT * P).rearrange("p (m j k q) -> p m j k q", m=3, j=KT, k=KT)
        wvo = take(KT * H).rearrange("p (k n) -> p k n", k=KT)
        xnT = take(KT * N).rearrange("p (k n) -> p k n", k=KT)
        qT = take(KT * N).rearrange("p (k n) -> p k n", k=KT)
        vo = take(NT * H).rearrange("p (i n) -> p i n", i=NT)
        probT = take(2 * N).rearrange("p (b j q) -> p b j q", b=2, j=NT)
        xin = sb("xin", [P, NT, H])
        prob = sb("prob", [P, 2, N])
        h = aT[:, :, :].rearrange("p f n -> p (f n)").rearrange("p (i n) -> p i n", i=NT)
        at = 0
        slot_in = take(PAIRS * ROW).rearrange("p (r c) -> p r c", r=PAIRS)
        slotT = take(KT * E * CAP).rearrange("p (k s) -> p k s", k=KT)
        ob = take(4 * 512).rearrange("p (b s) -> p b s", b=4)
        silu_c = h2T[:, 0, 0:256].rearrange("p (k n) -> p k n", k=KT)
        gabs = h2T[:, 0, 512:1024].rearrange("p (m n) -> p m n", m=2)
        tmpx = h2T[:, 1, 0:512].rearrange("p (b n) -> p b n", b=2)
        act_h = h2T[:, 0, 0:512].rearrange("p (b s) -> p b s", b=2)
        hid = h2T[:, 0, 512:1024].rearrange("p (b s) -> p b s", b=2)
        yin = [xin[:, 4 * b:4 * b + 4, :].rearrange("p a b -> p (a b)") for b in range(2)] + [
            prob[:, b, :] for b in range(2)]
        sh_act = prob[:, :, :].rearrange("p b n -> p (b n)").rearrange("p (b n) -> p b n", n=512)

        cc = sb("cc", [P, 4, KT])
        st = sb("st", [P, NT, 6])
        mv1 = sb("mv1", [P, NT, 2])
        mv2 = sb("mv2", [P, NT, 2])
        mv3 = sb("mv3", [P, NT, 2])
        rstd = sb("rstd", [P, 3, NT])
        nmr = sb("nmr", [P, NT])
        lnv = sb("lnv", [P, 3, NT])
        seed = sb("seed", [P, 3, NT])
        half_v = sb("half_v", [P, 3, NT])
        newt = sb("newt", [P, 3, NT])
        eps = sb("eps", [P, 1])
        rmax = sb("rmax", [P, NT])
        nmax = sb("nmax", [P, NT])
        rsum = sb("rsum", [P, NT])
        rinv = sb("rinv", [P, NT])
        BE = 2 * E
        r_ex = sb("r_ex", [P, BE])
        r_sc = sb("r_sc", [P, BE])
        score = sb("score", [P, BE])
        t_hi = sb("t_hi", [P, 2, GROUPS, 4])
        t_lo = sb("t_lo", [P, 2, GROUPS, 4])
        t_h2 = sb("t_h2", [P, 2, GROUPS, 2])
        t_m2 = sb("t_m2", [P, 2, GROUPS, 2])
        t_l2 = sb("t_l2", [P, 2, GROUPS, 2])
        t_3 = sb("t_3", [P, 4, 2, GROUPS])
        g_gt = sb("g_gt", [P, 2, GROUPS, GROUPS])
        g_ge = sb("g_ge", [P, 2, GROUPS, GROUPS])
        g_rank = sb("g_rank", [P, 2, GROUPS])
        chosen = sb("chosen", [P, 2, E])
        top8 = sb("top8", [P, 2, 8])
        idx8 = sb("idx8", [P, 2, 8], U32)
        hot = sb("hot", [P, 2, TOPK, E])
        hotx = sb("hotx", [P, 2, TOPK, E])
        mask_bf = sb("mask_bf", [P, NT, E], BF16)
        sk = sb("sk", [P, 2, TOPK])
        ssum = sb("ssum", [P, 2, 2])
        wk = sb("wk", [P, NT, TOPK])
        pk = sb("pk", [P, 2, TOPK])
        pbig = sb("pbig", [P, 2, TOPK])
        pidx = sb("pidx", [P, 2, TOPK])
        slot_idx = sb("slot_idx", [P, NT, TOPK], I32)
        m_eq = sb("m_eq", [P, 4, TOPK])
        m_row = sb("m_row", [P, 4])
        res_idx = sb("res_idx", [P, PAIRS], I32)

        c_loaded = sem("c_loaded")
        x_loaded = [sem(f"x_loaded{j}") for j in range(NB)]
        wmod_loaded = [sem("wmod_loaded0"), sem("wmod_loaded1")]
        qkv_loaded = sem("qkv_loaded")
        wo_loaded = sem("wo_loaded")
        small_loaded = sem("small_loaded")
        shared_loaded = sem("shared_loaded")
        experts_loaded = [sem(f"experts_loaded{g}") for g in range(4)]
        slots_zeroed = sem("slots_zeroed")
        results_zeroed = sem("results_zeroed")
        slots_loaded = [sem(f"slots_loaded{g}") for g in range(CHUNKS)]
        y_loaded = [sem(f"y_loaded{b}") for b in range(4)]
        out_stored = sem("out_stored")
        dispatched = sem("dispatched")
        returned = [sem(f"returned{b}") for b in range(4)]
        consts = sem("consts")
        dve_step = sem("dve_step")
        act_step = sem("act_step")
        cexp_done = sem("cexp_done")
        silu_c_done = sem("silu_c_done")
        mod_mm = sem("mod_mm")
        mod01 = sem("mod01")
        mod_raw = sem("mod_raw")
        gagb_done = sem("gagb_done")
        modc_mm = sem("modc_mm")
        modc_done = sem("modc_done")
        ring_filled = sem("ring_filled")
        ring_drained = sem("ring_drained")
        wqk_mm = sem("wqk_mm")
        wqk_done = sem("wqk_done")
        wvo_mm = sem("wvo_mm")
        wvo_done = sem("wvo_done")
        h_done = sem("h_done")
        hstat_done = sem("hstat_done")
        var_done = sem("var_done")
        seed_done = sem("seed_done")
        hn_done = sem("hn_done")
        rbase_h = sem("rbase_h")
        rbase_done = sem("rbase_done")
        qT_mm = sem("qT_mm")
        qT_act = sem("qT_act")
        qT_dve = sem("qT_dve")
        vo_mm = sem("vo_mm")
        vo_done = sem("vo_done")
        scores_mm = sem("scores_mm")
        nmax_done = sem("nmax_done")
        exp_done = sem("exp_done")
        pv_mm = sem("pv_mm")
        x2_done = sem("x2_done")
        rows_done = sem("rows_done")
        logits_mm = sem("logits_mm")
        gexp_done = sem("gexp_done")
        mask_done = sem("mask_done")
        pos_mm = sem("pos_mm")
        pos_read = sem("pos_read")
        sidx_done = sem("sidx_done")
        sh_mm = sem("sh_mm")
        sh_silu = sem("sh_silu")
        sh_hid = sem("sh_hid")
        shd_scaled = sem("shd_scaled")
        shd_mm = sem("shd_mm")
        base_done = sem("base_done")
        slotT_mm = sem("slotT_mm")
        slotT_act = sem("slotT_act")
        slotT_dve = sem("slotT_dve")
        ridx_done = sem("ridx_done")
        up_mm = sem("up_mm")
        silu_done = sem("silu_done")
        hid_done = sem("hid_done")
        down_mm = sem("down_mm")
        ob_done = sem("ob_done")
        final_done = sem("final_done")

        def ring_plan():
            plan = ["wT0", "wT1", "wT2", "gateT"] + [f"hn{j}" for j in range(NB)]
            for i in range(NT):
                plan += [f"p{i}.{g}" for g in range(i // 4 + 1)]
                if i >= 1:
                    plan.append(f"x{i - 1}")
            plan.append(f"x{NT - 1}")
            return {name: n for n, name in enumerate(plan)}

        ring = ring_plan()
        ring_bank = lambda name: bank[4 + ring[name] % 2]

        SH_ORDER = [(0, 0, 0), (0, 0, 1), (0, 1, 0), (0, 1, 1), (1, 0, 0), (1, 0, 1), (1, 1, 0), (1, 1, 1)]
        SH_COUNT = {key: n + 1 for n, key in enumerate(SH_ORDER)}
        SH_BANK = {key: bank[b] for key, b in zip(SH_ORDER, (0, 1, 2, 3, 6, 4, 5, 0))}
        SHD_BANK = [bank[b] for b in (1, 2, 3, 6)]
        esum = sb("esum", [P, NT, 2])
        bmax = sb("bmax", [P, NT, 2])

        RSQRT = [(0, 0, 4), (0, 4, 4)] + [(1, 2 * j, 2) for j in range(NB)] + [(2, i, 1) for i in range(NT)]
        MOMENTS = (mv1, mv2, mv3)

        block = ctx.enter_context(nc.Block())

        def store(sp, i):
            sp.wait_ge(final_done, i + 1)
            sp.dma_start(out_d[:, i, :], base[:, i, :]).then_inc(out_stored, 16)

        @block.sync
        def _(sp):
            sp.dma_start(cc[:, 0, :], c.rearrange("a (p k) -> p (a k)", k=KT)).then_inc(c_loaded, 16)
            wmod_d = wmod.rearrange("(p k) n -> p k n", k=KT)
            sp.dma_start(xin[:, 0:2, :], x_d[:, 0:2, :]).then_inc(x_loaded[0], 16)
            sp.dma_start(wmod_a, wmod_d[:, :, 0:512]).then_inc(wmod_loaded[0], 16)
            sp.dma_start(xin[:, 2:4, :], x_d[:, 2:4, :]).then_inc(x_loaded[1], 16)
            sp.dma_start(qkv_sb, qkv.rearrange("(p k) n -> p k n", k=KT)).then_inc(qkv_loaded, 16)
            sp.dma_start(xin[:, 4:6, :], x_d[:, 4:6, :]).then_inc(x_loaded[2], 16)
            sp.dma_start(wmod_b, wmod_d[:, :, 512:1536]).then_inc(wmod_loaded[1], 16)
            sp.dma_start(gb_col[:, 0, :], col(gamma)).then_inc(small_loaded, 16)
            sp.dma_start(gb_col[:, 1, :], col(beta)).then_inc(small_loaded, 16)
            sp.dma_start(gatew_sb[:, :], gate_w).then_inc(small_loaded, 16)
            sp.dma_start(bias_b[:, :], row_bcast(gate_bias)).then_inc(small_loaded, 16)
            sp.dma_start(wo_sb, o_proj.rearrange("(j p) n -> p j n", p=P)).then_inc(wo_loaded, 16)
            sp.dma_start(xin[:, 6:8, :], x_d[:, 6:8, :]).then_inc(x_loaded[3], 16)
            sp.wait_ge(consts, 1)
            z = prob[:, :, :].rearrange("p b n -> p (b n)")
            sp.dma_start(slots_d.rearrange("(p a) c -> p (a c)", p=P).rearrange("p (b n) -> p b n", n=2 * ROW),
                         z[:, 0:2 * ROW].unsqueeze(1).to_broadcast([P, 8, 2 * ROW])).then_inc(slots_zeroed, 16)
            sp.dma_start(shg_sb[:, :, :], shared_gate.rearrange("(p k) n -> p k n", k=KT)).then_inc(shared_loaded, 16)
            sp.dma_start(shu_sb[:, :, :], shared_up.rearrange("(p k) n -> p k n", k=KT)).then_inc(shared_loaded, 16)
            sp.dma_start(shd_sb[:, :, :], shared_down.rearrange("(j p) n -> p j n", p=P)).then_inc(shared_loaded, 16)
            sp.dma_start(results_d.rearrange("(p a) c -> p (a c)", p=P).rearrange("p (b n) -> p b n", n=N),
                         z[:, 0:N].unsqueeze(1).to_broadcast([P, 8, N])).then_inc(results_zeroed, 16)
            w = E // 4
            for g in range(4):
                e = slice(w * g, w * g + w)
                if g == 3:
                    sp.wait_ge(mod_mm, 3)
                    sp.wait_ge(wvo_mm, 1)
                    sp.wait_ge(qT_mm, 2)
                sp.dma_start(w1_sb[:, e], w1[e].rearrange("e (p k) f -> p e (k f)", k=KT)
                             .rearrange("p e (k f) -> p e k f", k=KT)).then_inc(experts_loaded[g], 16)
                sp.dma_start(w3_sb[:, e], w3[e].rearrange("e (p k) f -> p e (k f)", k=KT)
                             .rearrange("p e (k f) -> p e k f", k=KT)).then_inc(experts_loaded[g], 16)
                sp.dma_start(w2_sb[:, e], w2[e].rearrange("e p n -> p e n")).then_inc(experts_loaded[g], 16)
            sp.wait_ge(dispatched, 16 * TOPK * NT)
            for g in range(CHUNKS):
                sp.dma_start(slot_in[:, 4 * g:4 * g + 4, :], slots_rows[:, 4 * g:4 * g + 4, :])\
                  .then_inc(slots_loaded[g], 16)
            for b in range(4):
                sp.wait_ge(returned[b], 16 * PAIRS // 4)
            for i in range(NT):
                if i >= 4:
                    sp.wait_ge(final_done, i - 3)
                sp.dma_start(yin[i % 4], results_rows[:, i, :]).then_inc(y_loaded[i % 4], 16)
                if i >= 3:
                    store(sp, i - 3)
            for i in range(NT - 3, NT):
                store(sp, i)
            sp.wait_ge(out_stored, 16 * NT)

        @block.gpsimd
        def _(pool):
            g = nc.gpsimd
            g.memset(prob[:, :, :], 0.0).then_inc(consts, 1)
            g.memset(eps[:, :], LN_EPS)
            g.memset(ones_f[:, :], 1.0).then_inc(consts, 1)
            pool.wait_ge(consts, 2)
            g.affine_select(out=ident[:, :], in_=ones_f[:, :], pattern=[[-1, P]], compare_op=ALU.is_equal,
                            fill=0.0, base=0, channel_multiplier=1).then_inc(consts, 1)
            g.memset(ones_bf[:, :], 1.0).then_inc(consts, 1)
            pool.wait_ge(consts, 4)
            g.affine_select(out=ident_bf[:, :], in_=ones_bf[:, :], pattern=[[-1, P]], compare_op=ALU.is_equal,
                            fill=0.0, base=0, channel_multiplier=1).then_inc(consts, 1)
            g.affine_select(out=earlier_bf[:, :], in_=ones_bf[:, :], pattern=[[1, P]], compare_op=ALU.is_gt,
                            fill=0.0, base=0, channel_multiplier=-1).then_inc(consts, 1)
            g.memset(causal_bf[:, :], 0.0).then_inc(consts, 1)
            pool.wait_ge(consts, 7)
            g.affine_select(out=causal_bf[:, :], in_=causal_bf[:, :], pattern=[[-1, P]], compare_op=ALU.is_ge,
                            fill=MASKED, base=0, channel_multiplier=1).then_inc(consts, 1)
            lw = lower[:, :, :]
            g.affine_select(out=lw, in_=ones_f[:, 0:16].rearrange("p (a b) -> p a b", a=GROUPS),
                            pattern=[[1, GROUPS], [-1, GROUPS]], compare_op=ALU.is_gt, fill=0.0, base=0,
                            channel_multiplier=0).then_inc(consts, 1)
            g.iota(iota_i[:, 0:E], [[1, E]], base=1, channel_multiplier=0).then_inc(consts, 1)
            g.iota(iota_i[0:64, 32:32 + PAIRS], [[2, PAIRS]], base=1, channel_multiplier=0).then_inc(consts, 1)
            pool.wait_ge(consts, 11)
            g.iota(iota_i[64:128, 32:32 + PAIRS], [[2, PAIRS]], base=2, channel_multiplier=0).then_inc(consts, 1)
            pool.wait_ge(consts, 12)
            g.iota(iota_i[:, 64:64 + NT * TOPK], [[P * TOPK, NT], [1, TOPK]], base=-int(SKIP),
                   channel_multiplier=TOPK).then_inc(consts, 1)
            pool.wait_ge(consts, 13)
            g.tensor_copy(enum[:, :], iota_i[:, 0:E]).then_inc(consts, 1)
            g.tensor_copy(slot_expert[:, :], iota_i[:, 32:32 + PAIRS]).then_inc(consts, 1)
            g.tensor_copy(rows[:, :, H + TOPK:ROW],
                          iota_i[:, 64:64 + NT * TOPK].rearrange("p (i k) -> p i k", i=NT)).then_inc(consts, 1)
            pool.wait_ge(gagb_done, 1)
            for i in range(NT):
                pool.wait_ge(h_done, i + 1)
                g.tensor_tensor(base[:, i, :], h[:, i, :], mod[:, 2, :], ALU.mult).then_inc(rbase_h, 1)
                pool.wait_ge(rbase_h, i + 1)
                g.tensor_tensor(base[:, i, :], base[:, i, :], xin[:, i, :], ALU.add).then_inc(rbase_done, 1)
            pool.wait_ge(shared_loaded, 48)
            g.tensor_tensor(shd_sb[:, :, :], shd_sb[:, :, :],
                            mod[:, 5, :].unsqueeze(1).to_broadcast([P, FS // P, H]), ALU.mult).then_inc(shd_scaled, 1)
            pool.wait_ge(slots_zeroed, 16)
            for i in range(NT):
                if i % 2 == 0:
                    pool.wait_ge(sidx_done, i // 2 + 1)
                for k in range(TOPK):
                    g.indirect_dma_start(out=slots_d, out_offset=bass.IndirectOffsetOnAxis(
                        ap=slot_idx[:, i, k:k + 1], axis=0), in_=rows[:, i, :], in_offset=None,
                        bounds_check=E * CAP - 1, oob_is_err=False).then_inc(dispatched, 16)
            pool.wait_ge(results_zeroed, 16)
            for r in range(PAIRS):
                if r % 4 == 0:
                    pool.wait_ge(ridx_done, r // 4 + 1)
                if r % 2 == 0:
                    pool.wait_ge(ob_done, r // 2 + 1)
                g.indirect_dma_start(out=results_d, out_offset=bass.IndirectOffsetOnAxis(
                    ap=res_idx[:, r:r + 1], axis=0), in_=ob[:, (r // 2) % 4, (r % 2) * H:(r % 2 + 1) * H],
                    in_offset=None, bounds_check=N * TOPK - 1, oob_is_err=False).then_inc(returned[(r // 2) % 4], 16)

        @block.scalar
        def _(act):
            a = nc.scalar
            steps = [0]

            def settle(ins):
                steps[0] += 1
                ins.then_inc(act_step, 1)
                act.wait_ge(act_step, steps[0])

            def rsqrt_seed(n):
                which, first, count = RSQRT[n]
                r = slice(first, first + count)
                act.wait_ge(var_done, n + 1)
                settle(a.activation(lnv[:, which, r], MOMENTS[which][:, r, 1], ACT.Ln, bias=eps[:, 0:1]))
                a.activation(seed[:, which, r], lnv[:, which, r], ACT.Exp, scale=-0.5).then_inc(seed_done, 1)

            act.wait_ge(c_loaded, 16)
            a.activation(cc[:, 1, :], cc[:, 0, :], ACT.Exp, scale=-1.0).then_inc(cexp_done, 1)
            act.wait_ge(consts, 2)
            rsqrt_seed(0)
            rsqrt_seed(1)
            for m in range(3):
                act.wait_ge(ring_filled, ring[f"wT{m}"] + 1)
                a.copy(wT[:, m], ring_bank(f"wT{m}")[:, :].rearrange("p (j k q) -> p j k q", j=KT, k=KT))\
                 .then_inc(ring_drained, 1)
            rsqrt_seed(2)
            rsqrt_seed(3)
            for b in range(2):
                act.wait_ge(mod_mm, b + 2)
                a.copy(mod[:, 2 + 2 * b:4 + 2 * b, :], bank[1 + b][:, :].rearrange("p (m n) -> p m n", m=2))\
                 .then_inc(mod_raw, 1)
            act.wait_ge(ring_filled, ring["gateT"] + 1)
            a.copy(gateT[:, :, :], ring_bank("gateT")[:, 0:KT * E].rearrange("p (k e) -> p k e", k=KT))\
             .then_inc(ring_drained, 1)
            act.wait_ge(wqk_mm, 1)
            a.copy(wqk, bank[3][:, :].rearrange("p (k n) -> p k n", k=KT)).then_inc(wqk_done, 1)
            act.wait_ge(small_loaded, 64)

            def hn_tile(i):
                act.wait_ge(hstat_done, i // 2 + 1)
                if i >= 2:
                    act.wait_ge(ring_filled, ring[f"hn{i // 2 - 1}"] + 1)
                a.activation(hn[:, i % 2, :].rearrange("q (k p) -> q p k", k=KT),
                             h[:, i, :].rearrange("q (p k) -> q p k", k=KT), ACT.Identity,
                             bias=nmr[:, i:i + 1], scale=rstd[:, 1, i:i + 1]).then_inc(hn_done, 1)

            def xn_evac(j):
                act.wait_ge(ring_filled, ring[f"hn{j}"] + 1)
                for k in range(KT):
                    last = a.activation(xnT[:, k, 256 * j:256 * j + 256],
                                        ring_bank(f"hn{j}")[:, 256 * k:256 * k + 256], ACT.Identity,
                                        bias=gb_col[:, 1, k:k + 1], scale=gb_col[:, 0, k:k + 1])
                last.then_inc(ring_drained, 1)

            def q_evac(half):
                act.wait_ge(qT_mm, half + 1)
                a.copy(qT[:, 0, 512 * half:512 * half + 512], bank[1][:, :]).then_inc(qT_act, 1)

            def exp_tile(i):
                act.wait_ge(nmax_done, i + 1)
                n = P * (i + 1)
                if i == 0:
                    act.wait_ge(slots_zeroed, 16)
                    act.wait_ge(results_zeroed, 16)
                for b in range((n + 511) // 512):
                    w = min(512, n - 512 * b)
                    last = a.activation(prob[:, i % 2, 512 * b:512 * b + w], bank[2 * (i % 2) + b][:, 0:w], ACT.Exp,
                                        bias=nmax[:, i:i + 1], scale=SCALE, accum_out=esum[:, i, b:b + 1])
                last.then_inc(exp_done, 1)

            def p_evac(i):
                for g in range(i // 4 + 1):
                    act.wait_ge(ring_filled, ring[f"p{i}.{g}"] + 1)
                    if i >= 2:
                        act.wait_ge(pv_mm, i - 1)
                    w = min(4, i + 1 - 4 * g)
                    a.copy(probT[:, i % 2, 4 * g:4 * g + w, :],
                           ring_bank(f"p{i}.{g}")[:, 0:P * w].rearrange("p (j q) -> p j q", j=w))\
                     .then_inc(ring_drained, 1)

            def h2_evac(i):
                act.wait_ge(ring_filled, ring[f"x{i}"] + 1)
                if i == 0:
                    act.wait_ge(modc_done, 1)
                for k in range(KT):
                    last = a.activation(h2T[:, k, P * i:P * i + P], ring_bank(f"x{i}")[:, P * k:P * k + P],
                                        ACT.Identity, bias=modc[:, 1, k:k + 1], scale=modc[:, 0, k:k + 1])
                last.then_inc(ring_drained, 1)

            def gate_exp(b):
                act.wait_ge(logits_mm, b + 1)
                if b >= 1:
                    act.wait_ge(mask_done, b)
                a.activation(r_ex[:, :], bank[7][:, 0:BE], ACT.Exp, scale=-1.0).then_inc(gexp_done, 1)

            hn_tile(0)
            hn_tile(1)
            rsqrt_seed(4)
            xn_evac(0)
            hn_tile(2)
            hn_tile(3)
            xn_evac(1)
            rsqrt_seed(5)
            q_evac(0)
            hn_tile(4)
            hn_tile(5)
            exp_tile(0)
            xn_evac(2)
            hn_tile(6)
            hn_tile(7)
            xn_evac(3)
            q_evac(1)
            for i in range(NT):
                p_evac(i)
                if i % 2 == 1 and i >= 3:
                    gate_exp((i - 3) // 2)
                if i + 1 < NT:
                    exp_tile(i + 1)
                rsqrt_seed(6 + i)
                if i >= 1:
                    h2_evac(i - 1)
            h2_evac(NT - 1)
            gate_exp(NB - 1)
            for half in range(2):
                for ft in range(FS // P):
                    act.wait_ge(sh_mm, SH_COUNT[half, 0, ft])
                    a.activation(sh_act[:, ft + 2 * half, :], SH_BANK[half, 0, ft][:, :], ACT.Silu)\
                     .then_inc(sh_silu, 1)
            def slot_evac(g):
                act.wait_ge(slotT_mm, g + 1)
                a.activation(slotT[:, 0, 512 * g:512 * g + 512], bank[2 * (g % 2)][:, :], ACT.Identity,
                             bias=modc[:, 1, 0:1], scale=modc[:, 0, 0:1]).then_inc(slotT_act, 1)

            slot_evac(0)
            for g in range(EGROUPS):
                if g % 2 == 0 and g // 2 + 1 < CHUNKS:
                    slot_evac(g // 2 + 1)
                act.wait_ge(up_mm, g + 1)
                if g >= 2:
                    act.wait_ge(hid_done, g - 1)
                a.activation(act_h[:, g % 2, :], bank[4 + g % 2][:, 0:256], ACT.Silu).then_inc(silu_done, 1)

        @block.vector
        def _(dve):
            v = nc.vector
            steps = [0]

            def step(ins):
                steps[0] += 1
                ins.then_inc(dve_step, 1)

            def settle():
                dve.wait_ge(dve_step, steps[0])

            def chain(ins):
                step(ins)
                settle()

            dve.wait_ge(cexp_done, 1)
            chain(v.tensor_scalar(cc[:, 2, :], cc[:, 1, :], 1.0, None, ALU.add))
            chain(v.reciprocal(cc[:, 3, :], cc[:, 2, :]))
            chain(v.tensor_tensor(cc[:, 1, :], cc[:, 0, :], cc[:, 3, :], ALU.mult))
            v.tensor_copy(silu_c[:, :, :], cc[:, 1, :].unsqueeze(2).to_broadcast([P, KT, P])).then_inc(silu_c_done, 1)

            def moments(n, src):
                which, first, count = RSQRT[n]
                tiles, mv = range(first, first + count), MOMENTS[which]
                for i in tiles:
                    step(v.bn_stats(st[:, i, :], src[:, i, :]))
                settle()
                for i in tiles:
                    last = v.bn_aggr(mv[:, i, :], st[:, i, :])
                last.then_inc(var_done, 1)
                dve.wait_ge(var_done, n + 1)
                r = slice(first, first + count)
                step(v.tensor_scalar(half_v[:, which, r], mv[:, r, 1], LN_EPS, -0.5, ALU.add, ALU.mult))

            def refine(n):
                which, first, count = RSQRT[n]
                r = slice(first, first + count)
                dve.wait_ge(seed_done, n + 1)
                settle()
                chain(v.tensor_tensor(newt[:, which, r], half_v[:, which, r], seed[:, which, r], ALU.mult))
                chain(v.tensor_tensor(newt[:, which, r], newt[:, which, r], seed[:, which, r], ALU.mult))
                chain(v.scalar_tensor_tensor(out=rstd[:, which, r], in0=newt[:, which, r], scalar=1.5,
                                             in1=seed[:, which, r], op0=ALU.add, op1=ALU.mult))

            def x_moments(n):
                for j in (2 * n, 2 * n + 1):
                    dve.wait_ge(x_loaded[j], 16)
                moments(n, xin)

            def make_h(j):
                for i in (2 * j, 2 * j + 1):
                    step(v.scalar_tensor_tensor(out=tmpx[:, i % 2, :], in0=xin[:, i, :], scalar=mv1[:, i, 0:1],
                                                in1=mod[:, 1, :], op0=ALU.subtract, op1=ALU.mult))
                settle()
                for i in (2 * j, 2 * j + 1):
                    v.scalar_tensor_tensor(out=h[:, i, :], in0=tmpx[:, i % 2, :], scalar=rstd[:, 0, i:i + 1],
                                           in1=mod[:, 0, :], op0=ALU.mult, op1=ALU.add).then_inc(h_done, 1)
                dve.wait_ge(h_done, 2 * j + 2)
                moments(2 + j, h)

            def norm_h(j):
                refine(2 + j)
                r = slice(2 * j, 2 * j + 2)
                v.scalar_tensor_tensor(out=nmr[:, r], in0=mv2[:, r, 0], scalar=-1.0, in1=rstd[:, 1, r],
                                       op0=ALU.mult, op1=ALU.mult).then_inc(hstat_done, 1)

            def mod01_evac():
                dve.wait_ge(mod_mm, 1)
                v.tensor_copy(mod[:, 0, :], bank[0][:, 0:H])
                v.tensor_scalar(mod[:, 1, :], bank[0][:, H:2 * H], 1.0, None, ALU.add).then_inc(mod01, 1)
                dve.wait_ge(mod01, 1)

            def gates():
                dve.wait_ge(mod_raw, 2)
                both = mod[:, 2:6:3, :]
                chain(v.scalar_tensor_tensor(out=gabs[:, :, :], in0=both, scalar=-1.0, in1=both,
                                             op0=ALU.mult, op1=ALU.max))
                step(v.tensor_scalar(gabs[:, :, :], gabs[:, :, :], 0.25, None, ALU.max))
                chain(v.tensor_scalar(both, both, 0.0, 2.0, ALU.is_ge, ALU.mult))
                v.scalar_tensor_tensor(out=both, in0=both, scalar=1.0, in1=gabs[:, :, :],
                                       op0=ALU.subtract, op1=ALU.mult).then_inc(gagb_done, 1)
                dve.wait_ge(gagb_done, 1)

            def mod_columns():
                dve.wait_ge(modc_mm, 1)
                v.tensor_copy(modc[:, 1, :], bank[7][:, 0:KT])
                v.tensor_scalar(modc[:, 0, :], bank[7][:, KT:2 * KT], 1.0, None, ALU.add).then_inc(modc_done, 1)

            def wvo_evac():
                dve.wait_ge(wvo_mm, 1)
                v.tensor_tensor(wvo, bank[6][:, :].rearrange("p (k n) -> p k n", k=KT),
                                mod[:, 2, :].unsqueeze(1).to_broadcast([P, KT, H]), ALU.mult).then_inc(wvo_done, 1)

            def q_evac(half):
                dve.wait_ge(qT_mm, half + 1)
                v.tensor_copy(qT[:, 1, 512 * half:512 * half + 512], bank[3][:, :]).then_inc(qT_dve, 1)

            def vo_evac(j):
                dve.wait_ge(vo_mm, j + 1)
                v.tensor_copy(vo[:, 2 * j:2 * j + 2, :],
                              bank[6 + j % 2][:, :].rearrange("p (i n) -> p i n", i=2)).then_inc(vo_done, 1)

            def row_max(i):
                dve.wait_ge(scores_mm, i + 1)
                n = P * (i + 1)
                nb = (n + 511) // 512
                for b in range(nb):
                    w = min(512, n - 512 * b)
                    step(v.tensor_reduce(bmax[:, i, b:b + 1], bank[2 * (i % 2) + b][:, 0:w], AX_X, ALU.max))
                settle()
                if nb == 2:
                    chain(v.tensor_tensor(bmax[:, i, 0:1], bmax[:, i, 0:1], bmax[:, i, 1:2], ALU.max))
                v.tensor_scalar(nmax[:, i:i + 1], bmax[:, i, 0:1], -SCALE, None, ALU.mult).then_inc(nmax_done, 1)

            def add_attention(i):
                dve.wait_ge(exp_done, i + 1)
                if i >= 4:
                    chain(v.tensor_tensor(esum[:, i, 0:1], esum[:, i, 0:1], esum[:, i, 1:2], ALU.add))
                chain(v.reciprocal(rinv[:, i:i + 1], esum[:, i, 0:1]))
                dve.wait_ge(rbase_done, i + 1)
                dve.wait_ge(pv_mm, i + 1)
                v.scalar_tensor_tensor(out=base[:, i, :], in0=bank[6][:, 0:H], scalar=rinv[:, i:i + 1],
                                       in1=base[:, i, :], op0=ALU.mult, op1=ALU.add).then_inc(x2_done, 1)
                dve.wait_ge(x2_done, i + 1)
                moments(6 + i, base)

            def norm_x2(i):
                refine(6 + i)
                v.tensor_scalar(rows[:, i, 0:H].rearrange("q (k p) -> q p k", k=KT),
                                base[:, i, :].rearrange("q (p k) -> q p k", k=KT), mv3[:, i, 0:1],
                                rstd[:, 2, i:i + 1], ALU.subtract, ALU.mult).then_inc(rows_done, 1)

            def route_choose(b):
                g4 = lambda t: t.rearrange("p (t g e) -> p t g e", t=2, g=GROUPS)
                dve.wait_ge(gexp_done, b + 1)
                chain(v.tensor_scalar(r_sc[:, :], r_ex[:, :], 1.0, None, ALU.add))
                chain(v.reciprocal(score[:, :], r_sc[:, :]))
                chain(v.tensor_tensor(r_sc[:, :].rearrange("p (t e) -> p t e", t=2),
                                      score[:, :].rearrange("p (t e) -> p t e", t=2),
                                      bias_b[:, :].unsqueeze(1).to_broadcast([P, 2, E]), ALU.add))
                s = g4(r_sc[:, :])
                step(v.tensor_tensor(t_hi[:, :, :, :], s[:, :, :, 0:4], s[:, :, :, 4:8], ALU.max))
                chain(v.tensor_tensor(t_lo[:, :, :, :], s[:, :, :, 0:4], s[:, :, :, 4:8], ALU.min))
                step(v.tensor_tensor(t_h2[:, :, :, :], t_hi[:, :, :, 0:2], t_hi[:, :, :, 2:4], ALU.max))
                step(v.tensor_tensor(t_m2[:, :, :, :], t_hi[:, :, :, 0:2], t_hi[:, :, :, 2:4], ALU.min))
                chain(v.tensor_tensor(t_l2[:, :, :, :], t_lo[:, :, :, 0:2], t_lo[:, :, :, 2:4], ALU.max))
                step(v.tensor_tensor(t_3[:, 0], t_h2[:, :, :, 0], t_h2[:, :, :, 1], ALU.max))
                step(v.tensor_tensor(t_3[:, 1], t_h2[:, :, :, 0], t_h2[:, :, :, 1], ALU.min))
                chain(v.tensor_tensor(t_l2[:, :, :, :], t_l2[:, :, :, :], t_m2[:, :, :, :], ALU.max))
                chain(v.tensor_tensor(t_3[:, 2], t_l2[:, :, :, 0], t_l2[:, :, :, 1], ALU.max))
                chain(v.tensor_tensor(t_3[:, 2], t_3[:, 2], t_3[:, 1], ALU.max))
                chain(v.tensor_tensor(t_3[:, 3], t_3[:, 0], t_3[:, 2], ALU.add))
                gs = t_3[:, 3]
                other = gs.unsqueeze(2).to_broadcast([P, 2, GROUPS, GROUPS])
                own = gs.unsqueeze(3).to_broadcast([P, 2, GROUPS, GROUPS])
                step(v.tensor_tensor(g_gt[:, :, :, :], other, own, ALU.is_gt))
                chain(v.tensor_tensor(g_ge[:, :, :, :], other, own, ALU.is_ge))
                chain(v.tensor_tensor(g_ge[:, :, :, :], g_ge[:, :, :, :],
                                      lower[:, :, :].unsqueeze(1).to_broadcast([P, 2, GROUPS, GROUPS]), ALU.mult))
                chain(v.tensor_tensor(g_ge[:, :, :, :], g_ge[:, :, :, :], g_gt[:, :, :, :], ALU.max))
                chain(v.tensor_reduce(g_rank[:, :, :], g_ge[:, :, :, :], AX_X, ALU.add))
                chain(v.scalar_tensor_tensor(
                    out=chosen[:, :, :].rearrange("p t (g e) -> p t g e", g=GROUPS),
                    in0=g_rank[:, :, :].unsqueeze(3).to_broadcast([P, 2, GROUPS, EG]),
                    scalar=float(TOP_GROUPS), in1=s, op0=ALU.is_lt, op1=ALU.mult))
                for t in range(2):
                    step(v.max(top8[:, t, :], chosen[:, t, :]))
                settle()
                for t in range(2):
                    step(v.max_index(idx8[:, t, :], top8[:, t, :], chosen[:, t, :]))
                settle()
                chain(v.tensor_scalar(rows[:, 2 * b:2 * b + 2, H:H + TOPK], idx8[:, :, 0:TOPK], 1.0, None, ALU.add))
                chain(v.tensor_tensor(
                    hot[:, :, :, :], enum[:, :].unsqueeze(1).unsqueeze(1).to_broadcast([P, 2, TOPK, E]),
                    rows[:, 2 * b:2 * b + 2, H:H + TOPK].unsqueeze(3).to_broadcast([P, 2, TOPK, E]), ALU.is_equal))
                with nc.allow_low_precision("0 or 1"):
                    v.tensor_reduce(mask_bf[:, 2 * b:2 * b + 2, :], hot[:, :, :, :].rearrange("p t k e -> p t e k"),
                                    AX_X, ALU.add).then_inc(mask_done, 1)
                chain(v.tensor_tensor(hotx[:, :, :, :], hot[:, :, :, :],
                                      score[:, :].rearrange("p (t e) -> p t e", t=2).unsqueeze(2)
                                      .to_broadcast([P, 2, TOPK, E]), ALU.mult))
                chain(v.tensor_reduce(sk[:, :, :], hotx[:, :, :, :], AX_X, ALU.add))
                chain(v.tensor_reduce(ssum[:, :, 0], sk[:, :, :], AX_X, ALU.add))
                chain(v.tensor_scalar(ssum[:, :, 0], ssum[:, :, 0], 1e-20, None, ALU.add))
                chain(v.reciprocal(ssum[:, :, 1], ssum[:, :, 0]))
                step(v.scalar_tensor_tensor(out=wk[:, 2 * b:2 * b + 2, :], in0=sk[:, :, :], scalar=ROUTED_SCALE,
                                            in1=ssum[:, :, 1].unsqueeze(2).to_broadcast([P, 2, TOPK]),
                                            op0=ALU.mult, op1=ALU.mult))

            def route_place(b):
                dve.wait_ge(pos_mm, b + 1)
                v.tensor_tensor(hotx[:, :, :, :], hot[:, :, :, :],
                                bank[7][:, 64:64 + BE].rearrange("p (t e) -> p t e", t=2).unsqueeze(2)
                                .to_broadcast([P, 2, TOPK, E]), ALU.mult).then_inc(pos_read, 1)
                dve.wait_ge(pos_read, b + 1)
                chain(v.tensor_reduce(pk[:, :, :], hotx[:, :, :, :], AX_X, ALU.add))
                step(v.tensor_scalar(pbig[:, :, :], pk[:, :, :], float(CAP), SKIP, ALU.is_ge, ALU.mult))
                chain(v.scalar_tensor_tensor(out=pidx[:, :, :], in0=rows[:, 2 * b:2 * b + 2, H:H + TOPK],
                                             scalar=float(CAP), in1=pk[:, :, :], op0=ALU.mult, op1=ALU.add))
                v.scalar_tensor_tensor(out=slot_idx[:, 2 * b:2 * b + 2, :], in0=pidx[:, :, :], scalar=-float(CAP),
                                       in1=pbig[:, :, :], op0=ALU.add, op1=ALU.add).then_inc(sidx_done, 1)

            x_moments(0)
            x_moments(1)
            refine(0)
            mod01_evac()
            make_h(0)
            make_h(1)
            norm_h(0)
            refine(1)
            make_h(2)
            norm_h(1)
            gates()
            wvo_evac()
            mod_columns()
            make_h(3)
            q_evac(0)
            vo_evac(0)
            norm_h(2)
            vo_evac(1)
            norm_h(3)
            row_max(0)
            q_evac(1)
            vo_evac(2)
            vo_evac(3)
            dve.wait_ge(consts, 16)
            dve.wait_ge(small_loaded, 64)
            for i in range(NT):
                if i + 1 < NT:
                    row_max(i + 1)
                add_attention(i)
                if i >= 4 and i % 2 == 0:
                    route_place((i - 4) // 2)
                norm_x2(i)
                if i >= 3 and i % 2 == 1:
                    route_choose((i - 3) // 2)
            route_place(2)
            route_choose(3)
            for half in range(2):
                for ft in range(FS // P):
                    dve.wait_ge(sh_silu, 2 * half + ft + 1)
                    dve.wait_ge(sh_mm, SH_COUNT[half, 1, ft])
                    v.tensor_tensor(aT[:, ft, 512 * half:512 * half + 512], sh_act[:, ft + 2 * half, :],
                                    SH_BANK[half, 1, ft][:, :], ALU.mult).then_inc(sh_hid, 1)
                if half == 0:
                    route_place(3)
            for j in range(NB):
                dve.wait_ge(shd_mm, j + 1)
                v.tensor_tensor(base[:, 2 * j:2 * j + 2, :], SHD_BANK[j][:, :].rearrange("p (i n) -> p i n", i=2),
                                base[:, 2 * j:2 * j + 2, :], ALU.add).then_inc(base_done, 1)

            def slot_meta(g):
                dve.wait_ge(slots_loaded[g], 16)
                r = slice(4 * g, 4 * g + 4)
                chain(v.tensor_tensor(m_eq[:, :, :], slot_in[:, r, H:H + TOPK],
                                      slot_expert[:, r].unsqueeze(2).to_broadcast([P, 4, TOPK]), ALU.is_equal))
                chain(v.tensor_tensor(m_eq[:, :, :], m_eq[:, :, :], slot_in[:, r, H + TOPK:ROW], ALU.mult))
                chain(v.tensor_reduce(m_row[:, :], m_eq[:, :, :], AX_X, ALU.add))
                v.tensor_scalar(res_idx[:, r], m_row[:, :], SKIP, None, ALU.add).then_inc(ridx_done, 1)

            def slot_evac(g):
                dve.wait_ge(slotT_mm, g + 1)
                v.tensor_scalar(slotT[:, 1, 512 * g:512 * g + 512], bank[2 * (g % 2) + 1][:, :],
                                modc[:, 0, 1:2], modc[:, 1, 1:2], ALU.mult, ALU.add).then_inc(slotT_dve, 1)

            def expert_evac(g):
                dve.wait_ge(down_mm, g + 1)
                if g >= 4:
                    dve.wait_ge(returned[g % 4], 16 * 2 * (g // 4))
                v.tensor_tensor(ob[:, g % 4, :].rearrange("p (r n) -> p r n", r=2),
                                bank[6 + g % 2][:, :].rearrange("p (r n) -> p r n", r=2),
                                mod[:, 5, :].unsqueeze(1).to_broadcast([P, 2, H]), ALU.mult).then_inc(ob_done, 1)

            slot_evac(0)
            slot_meta(0)
            for g in range(EGROUPS):
                if g % 2 == 0 and g // 2 + 1 < CHUNKS:
                    slot_evac(g // 2 + 1)
                    slot_meta(g // 2 + 1)
                dve.wait_ge(silu_done, g + 1)
                if g >= 2:
                    dve.wait_ge(down_mm, g - 1)
                v.tensor_tensor(hid[:, g % 2, :], act_h[:, g % 2, :], bank[4 + g % 2][:, 256:512],
                                ALU.mult).then_inc(hid_done, 1)
                if g >= 1:
                    expert_evac(g - 1)
            expert_evac(EGROUPS - 1)
            for i in range(NT):
                dve.wait_ge(y_loaded[i % 4], 16 * (i // 4 + 1))
                for k in range(TOPK):
                    ins = v.scalar_tensor_tensor(out=base[:, i, :], in0=yin[i % 4][:, H * k:H * k + H],
                                                 scalar=wk[:, i, k:k + 1], in1=base[:, i, :],
                                                 op0=ALU.mult, op1=ALU.add)
                    if k < TOPK - 1:
                        chain(ins)
                ins.then_inc(final_done, 1)

        @block.tensor
        def _(pe):
            t = nc.tensor

            def ring_open(name):
                n = ring[name]
                if n >= 2:
                    pe.wait_ge(ring_drained, n - 1)
                return ring_bank(name)

            def product(dst, terms):
                for n, (lhsT, rhs) in enumerate(terms):
                    last = t.matmul(dst, lhsT, rhs, start=(n == 0), stop=(n == len(terms) - 1))
                return last

            def mod_rows(b):
                w = wmod_b[:, :, 512 * b - 512:512 * b] if b else wmod_a
                product(bank[b][:, :], [(silu_c[:, k, :], w[:, k, :]) for k in range(KT)])\
                    .then_inc(mod_mm, 1)

            pe.wait_ge(silu_c_done, 1)
            pe.wait_ge(wmod_loaded[0], 16)
            mod_rows(0)
            pe.wait_ge(consts, 3)
            pe.wait_ge(qkv_loaded, 16)
            for m in range(3):
                b = ring_open(f"wT{m}")
                for j in range(KT):
                    for k in range(KT):
                        o = P * (KT * j + k)
                        last = t.transpose(b[:, o:o + P], qkv_sb[:, k, H * m + P * j:H * m + P * j + P], ident[:, :])
                last.then_inc(ring_filled, 1)
            pe.wait_ge(wmod_loaded[1], 16)
            mod_rows(1)
            mod_rows(2)
            pe.wait_ge(small_loaded, 64)
            b = ring_open("gateT")
            for k in range(KT):
                last = t.transpose(b[:, E * k:E * k + E], gatew_sb[:, k::KT], ident[0:E, 0:E])
            last.then_inc(ring_filled, 1)
            pe.wait_ge(ring_drained, ring["wT1"] + 1)
            for k in range(KT):
                last = product(bank[3][:, H * k:H * k + H],
                               [(wT[:, 0, j, k, :], wT[:, 1, j].rearrange("p k q -> p (k q)")) for j in range(KT)])
            last.then_inc(wqk_mm, 1)
            pe.wait_ge(ring_drained, ring["wT2"] + 1)
            pe.wait_ge(wo_loaded, 16)
            for k in range(KT):
                last = product(bank[6][:, H * k:H * k + H], [(wT[:, 2, j, k, :], wo_sb[:, j, :]) for j in range(KT)])
            last.then_inc(wvo_mm, 1)
            pe.wait_ge(mod_raw, 2)
            for n, m in enumerate((3, 4)):
                for k in range(KT):
                    last = t.matmul(bank[7][:, KT * n + k:KT * n + k + 1], mod[0:1, m, k::KT], ones_f[0:1, 0:1],
                                    start=True, stop=True)
            last.then_inc(modc_mm, 1)

            def turn_h(j):
                pe.wait_ge(hn_done, 2 * j + 2)
                b = ring_open(f"hn{j}")
                for i in range(2):
                    for k in range(KT):
                        last = t.transpose(b[:, 256 * k + P * i:256 * k + P * i + P], hn[:, i, P * k:P * k + P],
                                           ident[:, :])
                last.then_inc(ring_filled, 1)

            def project_q(half):
                pe.wait_ge(ring_drained, ring[f"hn{2 * half + 1}"] + 1)
                pe.wait_ge(wqk_done, 1)
                pe.wait_ge(mod_raw, 1)
                if half:
                    pe.wait_ge(qT_act, 1)
                    pe.wait_ge(qT_dve, 1)
                for d in range(KT):
                    last = product(bank[1 + 2 * d][:, :], [(wqk[:, k, P * d:P * d + P],
                                                            xnT[:, k, 512 * half:512 * half + 512]) for k in range(KT)])
                last.then_inc(qT_mm, 1)

            def project_v(j):
                pe.wait_ge(ring_drained, ring[f"hn{j}"] + 1)
                pe.wait_ge(wvo_done, 1)
                pe.wait_ge(modc_done, 1)
                if j >= 2:
                    pe.wait_ge(vo_done, j - 1)
                for i in range(2):
                    tok = slice(256 * j + P * i, 256 * j + P * i + P)
                    last = product(bank[6 + j % 2][:, H * i:H * i + H], [(xnT[:, k, tok], wvo[:, k, :])
                                                                         for k in range(KT)])
                last.then_inc(vo_mm, 1)

            def scores(i):
                if i % 4 == 0:
                    pe.wait_ge(qT_act, i // 4 + 1)
                    pe.wait_ge(qT_dve, i // 4 + 1)
                if i >= 2:
                    pe.wait_ge(exp_done, i - 1)
                else:
                    pe.wait_ge(mod01, 1)
                    pe.wait_ge(mod_raw, 2)
                    pe.wait_ge(consts, 8)
                n = P * (i + 1)
                for b in range((n + 511) // 512):
                    w = min(512, n - 512 * b)
                    dst = bank[2 * (i % 2) + b]
                    t.matmul(dst[:, 0:w], qT[:, 0, P * i:P * i + P], xnT[:, 0, 512 * b:512 * b + w],
                             start=True, stop=False)
                    if b == i // 4:
                        t.matmul(dst[:, w - P:w], ident_bf[:, :], causal_bf[:, :], start=False, stop=False)
                    last = t.matmul(dst[:, 0:w], qT[:, 1, P * i:P * i + P], xnT[:, 1, 512 * b:512 * b + w],
                                    start=False, stop=True)
                last.then_inc(scores_mm, 1)

            def turn_p(i):
                pe.wait_ge(exp_done, i + 1)
                for g in range(i // 4 + 1):
                    b = ring_open(f"p{i}.{g}")
                    for j in range(4 * g, min(4 * g + 4, i + 1)):
                        last = t.transpose(b[:, P * (j - 4 * g):P * (j - 4 * g) + P], prob[:, i % 2, P * j:P * j + P],
                                           ident[:, :])
                    last.then_inc(ring_filled, 1)

            def weigh_v(i):
                pe.wait_ge(ring_drained, ring[f"p{i}.{i // 4}"] + 1)
                pe.wait_ge(vo_done, max(i // 2 + 1, 3))
                if i >= 1:
                    pe.wait_ge(x2_done, i)
                product(bank[6][:, 0:H], [(probT[:, i % 2, j, :], vo[:, j, :]) for j in range(i + 1)])\
                    .then_inc(pv_mm, 1)

            def turn_x(i):
                pe.wait_ge(rows_done, i + 1)
                b = ring_open(f"x{i}")
                for k in range(KT):
                    last = t.transpose(b[:, P * k:P * k + P], rows[:, i, P * k:P * k + P], ident[:, :])
                last.then_inc(ring_filled, 1)

            def logits(b):
                pe.wait_ge(ring_drained, ring[f"x{2 * b + 1}"] + 1)
                if b >= 1:
                    pe.wait_ge(gexp_done, b)
                    pe.wait_ge(pos_read, b)
                else:
                    pe.wait_ge(vo_done, NB)
                for i in range(2):
                    tok = slice(P * (2 * b + i), P * (2 * b + i) + P)
                    last = product(bank[7][:, E * i:E * i + E], [(h2T[:, k, tok], gateT[:, k, :]) for k in range(KT)])
                last.then_inc(logits_mm, 1)

            def positions(b):
                pe.wait_ge(mask_done, b + 1)
                for i in range(2 * b, 2 * b + 2):
                    o = 64 + E * (i - 2 * b)
                    last = product(bank[7][:, o:o + E], [(earlier_bf[:, :], mask_bf[:, i, :])]
                                   + [(ones_bf[:, :], mask_bf[:, j, :]) for j in range(i)])
                last.then_inc(pos_mm, 1)

            def shared_up_part(key):
                half, what, ft = key
                w = (shg_sb, shu_sb)[what]
                product(SH_BANK[key][:, :], [(w[:, k, P * ft:P * ft + P], h2T[:, k, 512 * half:512 * half + 512])
                                             for k in range(KT)]).then_inc(sh_mm, 1)

            turn_h(0)
            turn_h(1)
            project_q(0)
            project_v(0)
            project_v(1)
            scores(0)
            scores(1)
            turn_h(2)
            turn_h(3)
            project_q(1)
            project_v(2)
            project_v(3)
            for i in range(NT):
                turn_p(i)
                if i >= 3 and i % 2 == 1:
                    logits((i - 3) // 2)
                if i >= 4 and i % 2 == 0:
                    positions((i - 4) // 2)
                weigh_v(i)
                if i + 2 < NT:
                    scores(i + 2)
                if i >= 1:
                    turn_x(i - 1)
            pe.wait_ge(shared_loaded, 48)
            shared_up_part((0, 0, 0))
            shared_up_part((0, 0, 1))
            positions(2)
            turn_x(NT - 1)
            shared_up_part((0, 1, 0))
            logits(3)
            shared_up_part((0, 1, 1))
            pe.wait_ge(x2_done, NT)
            shared_up_part((1, 0, 0))
            pe.wait_ge(ring_drained, ring[f"x{NT - 1}"] + 1)
            shared_up_part((1, 0, 1))
            shared_up_part((1, 1, 0))
            pe.wait_ge(sh_silu, 1)
            shared_up_part((1, 1, 1))
            positions(3)
            pe.wait_ge(shd_scaled, 1)
            for j in range(NB):
                pe.wait_ge(sh_hid, (2, 2, 4, 4)[j])
                if j < 3:
                    pe.wait_ge(sh_silu, 2)
                for i in range(2):
                    tok = slice(P * (2 * j + i), P * (2 * j + i) + P)
                    last = product(SHD_BANK[j][:, H * i:H * i + H], [(aT[:, f, tok], shd_sb[:, f, :])
                                                                     for f in range(FS // P)])
                last.then_inc(shd_mm, 1)

            def turn_slots(g):
                pe.wait_ge(slots_loaded[g], 16)
                if g >= 2:
                    pe.wait_ge(slotT_act, g - 1)
                    pe.wait_ge(slotT_dve, g - 1)
                else:
                    pe.wait_ge(base_done, NB)
                    pe.wait_ge(sh_hid, 4)
                for k in range(KT):
                    for r in range(4):
                        last = t.transpose(bank[2 * (g % 2) + k][:, P * r:P * r + P],
                                           slot_in[:, 4 * g + r, P * k:P * k + P], ident[:, :])
                last.then_inc(slotT_mm, 1)

            def expert_up(g):
                if g % 2 == 0:
                    pe.wait_ge(experts_loaded[g // 2], 48)
                    pe.wait_ge(slotT_act, g // 2 + 1)
                    pe.wait_ge(slotT_dve, g // 2 + 1)
                if g >= 2:
                    pe.wait_ge(hid_done, g - 1)
                for what, w in enumerate((w1_sb, w3_sb)):
                    for n in range(4):
                        e = 4 * g + n
                        o = 256 * what + CAP * n
                        last = product(bank[4 + g % 2][:, o:o + CAP],
                                       [(w[:, e, k, :], slotT[:, k, CAP * e:CAP * e + CAP]) for k in range(KT)])
                last.then_inc(up_mm, 1)

            def expert_down(g):
                pe.wait_ge(hid_done, g + 1)
                if g >= 2:
                    pe.wait_ge(ob_done, g - 1)
                for n in range(4):
                    e = 4 * g + n
                    last = t.matmul(bank[6 + g % 2][CAP * (n % 2):CAP * (n % 2) + CAP, H * (n // 2):H * (n // 2) + H],
                                    hid[:, g % 2, CAP * n:CAP * n + CAP], w2_sb[:, e, :], start=True, stop=True)
                last.then_inc(down_mm, 1)

            turn_slots(0)
            for g in range(EGROUPS):
                if g % 2 == 0 and g // 2 + 1 < CHUNKS:
                    turn_slots(g // 2 + 1)
                expert_up(g)
                if g >= 1:
                    expert_down(g - 1)
            expert_down(EGROUPS - 1)


_INS = ['L0_attn_x', 'L0_attn_qkv', 'L0_attn_o_proj', 'L0_attn_gamma', 'L0_attn_beta', 'L0_ffn_gate_w',
        'L0_ffn_gate_bias', 'L0_ffn_w1', 'L0_ffn_w2', 'L0_ffn_w3', 'L0_ffn_shared_gate', 'L0_ffn_shared_up',
        'L0_ffn_shared_down', 'L0_c', 'L0_wmod']


def kernel(**inputs):
    import numpy as _np
    import concourse.bacc as _bacc
    from concourse import mybir as _mybir
    from concourse.bass_utils import run_bass_kernel_spmd as _run

    nc = _bacc.Bacc("TRN2", target_bir_lowering=False, num_devices=1)
    arrays, args = {}, []
    for name in _INS:
        a = _np.ascontiguousarray(inputs[name])
        arrays[f"in_{name}_dram"] = a
        args.append(nc.dram_tensor(f"in_{name}_dram", a.shape, _mybir.dt.from_np(a.dtype), kind="ExternalInput").ap())
    shape = inputs['L0_attn_x'].shape
    args.append(nc.dram_tensor("out_0_dram", shape, _mybir.dt.from_np(_np.dtype("float32")),
                               kind="ExternalOutput").ap())
    adaln_attention_moe(nc, *args)
    r = _run(nc, [arrays], core_ids=[0])
    return r.results[0]["out_0_dram"]
```

```python
from contextlib import ExitStack

import concourse.bass as bass
from concourse import mybir

P = 128
ALU = mybir.AluOpType
ACT = mybir.ActivationFunctionType
AX_X = mybir.AxisListType.X
F32 = mybir.dt.float32
BF16 = mybir.dt.bfloat16
I32 = mybir.dt.int32
U32 = mybir.dt.uint32

LN_EPS = 1e-5
TOPK = 4
GROUPS = 4
TOP_GROUPS = 2
ROUTED_SCALE = 2.0
CAP = 2 * (2 * 128 * TOPK // 32)
MASKED = -1e30
EXP_LN_TABLES = 6
SKIP = 8192.0


def adaln_attention_moe(nc, x, qkv, o_proj, gamma, beta, gate_w, gate_bias, w1, w2, w3,
                        shared_gate, shared_up, shared_down, c, wmod, out):
    _, N, H = x.shape
    E, _, F = w1.shape
    FS = shared_gate.shape[1]
    KT = H // P
    NT = N // P
    NB = NT // 2
    EG = E // GROUPS
    PAIRS = E // 2
    CHUNKS = PAIRS // 4
    EGROUPS = PAIRS // 2
    ROW = H + 2 * TOPK
    SCALE = float(H) ** -0.5
    BATCHES = [(0, 3), (3, 2), (5, 2), (7, 1)]
    TB = 3
    assert (H, F, FS, CAP, KT, NT, E) == (256, 128, 256, 64, 2, 8, 32)

    x_d = x.rearrange("b (i p) h -> p (b i) h", p=P)
    out_d = out.rearrange("b (i p) h -> p (b i) h", p=P)
    col = lambda v: v.rearrange("(p k) -> p k", k=KT)
    row_bcast = lambda v: v.rearrange("(a n) -> a n", a=1).to_broadcast([P, v.shape[0]])
    slots_d = nc.dram_tensor("slots", (E * CAP, ROW), F32).ap()
    results_d = nc.dram_tensor("results", (N * TOPK, H), F32).ap()
    slots_rows = slots_d.rearrange("(r p) c -> p r c", p=P)
    results_rows = results_d.rearrange("(i p k) h -> p i (k h)", p=P, k=TOPK)

    with ExitStack() as ctx:
        sb = lambda name, shape, dt=F32: ctx.enter_context(nc.sbuf_tensor(name, shape, dt))
        sem = lambda name: ctx.enter_context(nc.semaphore(name))
        bank = [ctx.enter_context(nc.psum_tensor(f"bank{i}", [P, 512], F32)) for i in range(8)]

        w1_sb = sb("w1_sb", [P, E, KT, F])
        w3_sb = sb("w3_sb", [P, E, KT, F])
        w2_sb = sb("w2_sb", [P, E, H])
        shg_sb = sb("shg_sb", [P, KT, FS])
        shu_sb = sb("shu_sb", [P, KT, FS])
        shd_sb = sb("shd_sb", [P, FS // P, H])
        bias_b = sb("bias_b", [P, E])
        gatew_sb = sb("gatew_sb", [E, H])
        gateT = sb("gateT", [P, KT, E])
        gb_col = sb("gb_col", [P, 2, KT])
        ident = sb("ident", [P, P])
        ident_bf = sb("ident_bf", [P, P], BF16)
        causal_bf = sb("causal_bf", [P, P], BF16)
        earlier_bf = sb("earlier_bf", [P, P], BF16)
        ones_bf = sb("ones_bf", [P, P], BF16)
        ones_f = sb("ones_f", [P, P])
        iota_i = sb("iota_i", [P, 128], I32)
        enum = sb("enum", [P, E])
        slot_expert = sb("slot_expert", [P, PAIRS])
        lower = sb("lower", [P, GROUPS, GROUPS])

        base = sb("base", [P, NT, H])
        rows = sb("rows", [P, NT, ROW])
        h2T = sb("h2T", [P, KT, N])
        aT = sb("aT", [P, FS // P, N])
        mod = sb("mod", [P, 6, H])
        modc = sb("modc", [P, 2, KT])

        last_q = slice(3 * E // 4, E)
        flat = lambda t, k: t.rearrange("p e k f -> p (e k f)") if k else t.rearrange("p e n -> p (e n)")
        place1, place3, place2 = flat(w1_sb[:, last_q], 1), flat(w3_sb[:, last_q], 1), flat(w2_sb[:, last_q], 0)
        wmod_a = place3[:, 0:1024].rearrange("p (k n) -> p k n", k=KT)
        wmod_b = place1.rearrange("p (k n) -> p k n", k=KT)
        wo_sb = place3[:, 1024:1536].rearrange("p (k n) -> p k n", k=KT)
        hn = rows[:, :, 0:H]
        qkv_sb = place2[:, 0:1536].rearrange("p (k n) -> p k n", k=KT)
        wqk = place2[:, 1536:2048].rearrange("p (k n) -> p k n", k=KT)

        ARENA = 10368
        arena = sb("arena", [P, ARENA])
        at = 0

        def take(n):
            nonlocal at
            at += n
            assert at <= ARENA
            return arena[:, at - n:at]

        wT = take(3 * KT * KT * P).rearrange("p (m j k q) -> p m j k q", m=3, j=KT, k=KT)
        wvo = take(KT * H).rearrange("p (k n) -> p k n", k=KT)
        xnT = take(KT * N).rearrange("p (k n) -> p k n", k=KT)
        qT = take(KT * N).rearrange("p (k n) -> p k n", k=KT)
        vo = take(NT * H).rearrange("p (i n) -> p i n", i=NT)
        probT = take(2 * N).rearrange("p (b j q) -> p b j q", b=2, j=NT)
        xin = sb("xin", [P, NT, H])
        prob = sb("prob", [P, 2, N])
        h = aT[:, :, :].rearrange("p f n -> p (f n)").rearrange("p (i n) -> p i n", i=NT)
        at = 0
        slot_in = take(PAIRS * ROW).rearrange("p (r c) -> p r c", r=PAIRS)
        slotT = take(KT * E * CAP).rearrange("p (k s) -> p k s", k=KT)
        ob = take(4 * 512).rearrange("p (b s) -> p b s", b=4)
        silu_c = h2T[:, 0, 0:256].rearrange("p (k n) -> p k n", k=KT)
        gabs = h2T[:, 0, 512:1024].rearrange("p (m n) -> p m n", m=2)
        act_h = h2T[:, 0, 0:512].rearrange("p (b r f) -> p b r f", b=2, r=2)
        hid = h2T[:, 0, 512:1024].rearrange("p (b r f) -> p b r f", b=2, r=2)
        hidT = prob[:, 1, 0:512].rearrange("p (b r s) -> p b r s", b=2, r=2)
        diag = [aT[:, n // 8, P * (n % 8):P * (n % 8) + P] for n in range(2 * NT)] + [
            h2T[:, 1, P * n:P * n + P] for n in range(NT)]
        hot = xin[:, 0:4, :].rearrange("p a b -> p (a b)").rearrange("p (t k e) -> p t k e", t=NT, k=TOPK)
        hotx = xin[:, 4:6, :].rearrange("p a b -> p (a b)").rearrange("p (t k e) -> p t k e", t=4, k=TOPK)
        score = xin[:, 6, :].rearrange("p (t e) -> p t e", t=NT)
        yin = [w1_sb[:, 4 * i:4 * i + 4].rearrange("p e k f -> p (e k f)") for i in range(NT)]
        sh_act = prob[:, :, :].rearrange("p b n -> p (b n)").rearrange("p (b n) -> p b n", n=512)

        cc = sb("cc", [P, 4, KT])
        st = sb("st", [P, NT, 6])
        mv1 = sb("mv1", [P, NT, 2])
        mv2 = sb("mv2", [P, NT, 2])
        mv3 = sb("mv3", [P, NT, 2])
        rstd = sb("rstd", [P, 3, NT])
        nmr = sb("nmr", [P, 2, NT])
        lnv = sb("lnv", [P, 3, NT])
        seed = sb("seed", [P, 3, NT])
        half_v = sb("half_v", [P, 3, NT])
        newt = sb("newt", [P, 3, NT])
        eps = sb("eps", [P, 1])
        nmax = sb("nmax", [P, NT])
        rsum = sb("rsum", [P, NT])
        rinv = sb("rinv", [P, NT])
        r_ex = sb("r_ex", [P, TB, E])
        r_sc = sb("r_sc", [P, TB, E])
        g_top = sb("g_top", [P, TB, GROUPS, EG])
        g_sum = sb("g_sum", [P, TB, GROUPS])
        g_cmp = sb("g_cmp", [P, TB, GROUPS, 2 * GROUPS])
        g_rank = sb("g_rank", [P, TB, GROUPS])
        chosen = sb("chosen", [P, TB, E])
        top8 = sb("top8", [P, TB, 8])
        idx8 = sb("idx8", [P, TB, 8], U32)
        mask_bf = sb("mask_bf", [P, NT, E], BF16)
        sk = sb("sk", [P, NT, TOPK])
        ssum = sb("ssum", [P, NT, 2])
        wk = sb("wk", [P, NT, TOPK])
        pk = sb("pk", [P, TB, TOPK])
        pbig = sb("pbig", [P, TB, TOPK])
        pidx = sb("pidx", [P, TB, TOPK])
        slot_idx = sb("slot_idx", [P, NT, TOPK], I32)
        m_eq = sb("m_eq", [P, 4, TOPK])
        m_row = sb("m_row", [P, 4])
        res_idx = sb("res_idx", [P, PAIRS], I32)

        c_loaded = sem("c_loaded")
        x_loaded = [sem(f"x_loaded{j}") for j in range(NB)]
        wmod_loaded = [sem("wmod_loaded0"), sem("wmod_loaded1")]
        qkv_loaded = sem("qkv_loaded")
        wo_loaded = sem("wo_loaded")
        small_loaded = sem("small_loaded")
        shared_loaded = sem("shared_loaded")
        experts_loaded = [sem(f"experts_loaded{g}") for g in range(4)]
        slots_zeroed = sem("slots_zeroed")
        results_zeroed = sem("results_zeroed")
        slots_loaded = [sem(f"slots_loaded{g}") for g in range(CHUNKS)]
        y_loaded = [sem(f"y_loaded{i}") for i in range(NT)]
        out_stored = sem("out_stored")
        dispatched = sem("dispatched")
        returned = [sem(f"returned{b}") for b in range(4)]
        consts = sem("consts")
        dve_step = sem("dve_step")
        act_step = sem("act_step")
        cexp_done = sem("cexp_done")
        silu_c_done = sem("silu_c_done")
        mod_mm = sem("mod_mm")
        mod01 = sem("mod01")
        mod_raw = sem("mod_raw")
        gagb_done = sem("gagb_done")
        modc_mm = sem("modc_mm")
        modc_done = sem("modc_done")
        ring_filled = sem("ring_filled")
        ring_drained = sem("ring_drained")
        wqk_mm = sem("wqk_mm")
        wqk_done = sem("wqk_done")
        wvo_mm = sem("wvo_mm")
        wvo_done = sem("wvo_done")
        h_dve = sem("h_dve")
        h_pool = sem("h_pool")
        xstat_done = sem("xstat_done")
        xhat_done = sem("xhat_done")
        xhat_scaled = sem("xhat_scaled")
        hstat_done = sem("hstat_done")
        var_done = sem("var_done")
        seed_done = sem("seed_done")
        hn_done = sem("hn_done")
        rbase_h = sem("rbase_h")
        rbase_done = sem("rbase_done")
        qT_mm = sem("qT_mm")
        qT_act = sem("qT_act")
        qT_dve = sem("qT_dve")
        vo_mm = sem("vo_mm")
        vo_done = sem("vo_done")
        scores_mm = sem("scores_mm")
        nmax_done = sem("nmax_done")
        exp_done = sem("exp_done")
        pv_mm = sem("pv_mm")
        x2_done = sem("x2_done")
        rows_done = sem("rows_done")
        logits_mm = sem("logits_mm")
        gexp_done = sem("gexp_done")
        score_done = sem("score_done")
        mask_done = sem("mask_done")
        pos_mm = sem("pos_mm")
        pos_read = sem("pos_read")
        sidx_done = sem("sidx_done")
        weights_done = sem("weights_done")
        sh_mm = sem("sh_mm")
        sh_silu = sem("sh_silu")
        sh_hid = sem("sh_hid")
        shd_scaled = sem("shd_scaled")
        shd_mm = sem("shd_mm")
        base_done = sem("base_done")
        slotT_mm = sem("slotT_mm")
        slotT_act = sem("slotT_act")
        slotT_dve = sem("slotT_dve")
        ridx_done = sem("ridx_done")
        up_mm = sem("up_mm")
        silu_done = sem("silu_done")
        hid_done = sem("hid_done")
        hidT_mm = sem("hidT_mm")
        hidT_done = sem("hidT_done")
        diag_done = sem("diag_done")
        sum_mm = sem("sum_mm")
        down_mm = sem("down_mm")
        ob_done = sem("ob_done")
        final_done = sem("final_done")

        def ring_plan():
            plan = ["wT0", "wT1", "wT2", "hn0", "hn1", "gateT", "hn2", "hn3"]
            for i in range(NT):
                plan += [f"p{i}.{g}" for g in range(i // 4 + 1)]
                if i >= 1:
                    plan.append(f"x{i - 1}")
            plan.append(f"x{NT - 1}")
            return {name: n for n, name in enumerate(plan)}

        ring = ring_plan()
        ring_bank = lambda name: bank[4 + ring[name] % 2]

        SH_ORDER = [(0, 0, 0), (0, 0, 1), (0, 1, 0), (0, 1, 1), (1, 0, 0), (1, 0, 1), (1, 1, 0), (1, 1, 1)]
        SH_COUNT = {key: n + 1 for n, key in enumerate(SH_ORDER)}
        SH_BANK = {key: bank[b] for key, b in zip(SH_ORDER, (0, 1, 2, 3, 6, 4, 5, 0))}
        SHD_BANK = [bank[b] for b in (1, 2, 3, 6)]
        esum = sb("esum", [P, NT, 2])
        bmax = sb("bmax", [P, NT, 2])

        RSQRT = [(0, 0, 4), (0, 4, 4)] + [(1, 2 * j, 2) for j in range(NB)] + [(2, i, 1) for i in range(NT)]
        MOMENTS = (mv1, mv2, mv3)

        scaled_by_pool = lambda i: sum(1 for tile in range(i + 1) if tile % 4)
        POS = 128
        MOD_BANK = [bank[b] for b in (0, 2, 7)]

        block = ctx.enter_context(nc.Block())

        def store(sp, i):
            sp.wait_ge(final_done, i + 1)
            sp.dma_start(out_d[:, i, :], base[:, i, :]).then_inc(out_stored, 16)

        @block.sync
        def _(sp):
            sp.dma_start(cc[:, 0, :], c.rearrange("a (p k) -> p (a k)", k=KT)).then_inc(c_loaded, 16)
            wmod_d = wmod.rearrange("(p k) n -> p k n", k=KT)
            for j in range(NB):
                sp.dma_start(xin[:, 2 * j:2 * j + 2, :], x_d[:, 2 * j:2 * j + 2, :]).then_inc(x_loaded[j], 16)
                if j == 1:
                    sp.dma_start(wmod_a, wmod_d[:, :, 0:512]).then_inc(wmod_loaded[0], 16)
            sp.dma_start(qkv_sb, qkv.rearrange("(p k) n -> p k n", k=KT)).then_inc(qkv_loaded, 16)
            sp.dma_start(wmod_b, wmod_d[:, :, 512:1536]).then_inc(wmod_loaded[1], 16)
            sp.dma_start(gb_col[:, 0, :], col(gamma)).then_inc(small_loaded, 16)
            sp.dma_start(gb_col[:, 1, :], col(beta)).then_inc(small_loaded, 16)
            sp.dma_start(gatew_sb[:, :], gate_w).then_inc(small_loaded, 16)
            sp.dma_start(bias_b[:, :], row_bcast(gate_bias)).then_inc(small_loaded, 16)
            sp.dma_start(wo_sb, o_proj.rearrange("(j p) n -> p j n", p=P)).then_inc(wo_loaded, 16)
            sp.wait_ge(consts, 1)
            z = prob[:, :, :].rearrange("p b n -> p (b n)")
            sp.dma_start(slots_d.rearrange("(p a) c -> p (a c)", p=P).rearrange("p (b n) -> p b n", n=2 * ROW),
                         z[:, 0:2 * ROW].unsqueeze(1).to_broadcast([P, 8, 2 * ROW])).then_inc(slots_zeroed, 16)
            sp.dma_start(shg_sb[:, :, :], shared_gate.rearrange("(p k) n -> p k n", k=KT)).then_inc(shared_loaded, 16)
            sp.dma_start(shu_sb[:, :, :], shared_up.rearrange("(p k) n -> p k n", k=KT)).then_inc(shared_loaded, 16)
            sp.dma_start(shd_sb[:, :, :], shared_down.rearrange("(j p) n -> p j n", p=P)).then_inc(shared_loaded, 16)
            sp.dma_start(results_d.rearrange("(p a) c -> p (a c)", p=P).rearrange("p (b n) -> p b n", n=N),
                         z[:, 0:N].unsqueeze(1).to_broadcast([P, 8, N])).then_inc(results_zeroed, 16)
            w = E // 4
            for g in range(4):
                e = slice(w * g, w * g + w)
                if g == 3:
                    sp.wait_ge(mod_mm, 3)
                    sp.wait_ge(wvo_mm, 1)
                    sp.wait_ge(qT_mm, 2)
                sp.dma_start(w1_sb[:, e], w1[e].rearrange("e (p k) f -> p e (k f)", k=KT)
                             .rearrange("p e (k f) -> p e k f", k=KT)).then_inc(experts_loaded[g], 16)
                sp.dma_start(w3_sb[:, e], w3[e].rearrange("e (p k) f -> p e (k f)", k=KT)
                             .rearrange("p e (k f) -> p e k f", k=KT)).then_inc(experts_loaded[g], 16)
                sp.dma_start(w2_sb[:, e], w2[e].rearrange("e p n -> p e n")).then_inc(experts_loaded[g], 16)
            sp.wait_ge(dispatched, 16 * TOPK * NT)
            for g in range(CHUNKS):
                sp.dma_start(slot_in[:, 4 * g:4 * g + 4, :], slots_rows[:, 4 * g:4 * g + 4, :])\
                  .then_inc(slots_loaded[g], 16)
            for b in range(4):
                sp.wait_ge(returned[b], 16 * PAIRS // 4)
            for i in range(NT):
                sp.dma_start(yin[i], results_rows[:, i, :]).then_inc(y_loaded[i], 16)
            for i in range(NT):
                store(sp, i)
            sp.wait_ge(out_stored, 16 * NT)

        @block.gpsimd
        def _(pool):
            g = nc.gpsimd
            g.memset(prob[:, :, :], 0.0).then_inc(consts, 1)
            g.memset(eps[:, :], LN_EPS)
            g.memset(ones_f[:, :], 1.0).then_inc(consts, 1)
            pool.wait_ge(consts, 2)
            g.affine_select(out=ident[:, :], in_=ones_f[:, :], pattern=[[-1, P]], compare_op=ALU.is_equal,
                            fill=0.0, base=0, channel_multiplier=1).then_inc(consts, 1)
            g.memset(ones_bf[:, :], 1.0).then_inc(consts, 1)
            pool.wait_ge(consts, 4)
            g.affine_select(out=ident_bf[:, :], in_=ones_bf[:, :], pattern=[[-1, P]], compare_op=ALU.is_equal,
                            fill=0.0, base=0, channel_multiplier=1).then_inc(consts, 1)
            g.affine_select(out=earlier_bf[:, :], in_=ones_bf[:, :], pattern=[[1, P]], compare_op=ALU.is_gt,
                            fill=0.0, base=0, channel_multiplier=-1).then_inc(consts, 1)
            g.memset(causal_bf[:, :], 0.0).then_inc(consts, 1)
            pool.wait_ge(consts, 7)
            g.affine_select(out=causal_bf[:, :], in_=causal_bf[:, :], pattern=[[-1, P]], compare_op=ALU.is_ge,
                            fill=MASKED, base=0, channel_multiplier=1).then_inc(consts, 1)
            lw = lower[:, :, :]
            g.affine_select(out=lw, in_=ones_f[:, 0:16].rearrange("p (a b) -> p a b", a=GROUPS),
                            pattern=[[1, GROUPS], [-1, GROUPS]], compare_op=ALU.is_gt, fill=0.0, base=0,
                            channel_multiplier=0).then_inc(consts, 1)
            g.iota(iota_i[:, 0:E], [[1, E]], base=1, channel_multiplier=0).then_inc(consts, 1)
            g.iota(iota_i[0:64, 32:32 + PAIRS], [[2, PAIRS]], base=1, channel_multiplier=0).then_inc(consts, 1)
            pool.wait_ge(consts, 11)
            g.iota(iota_i[64:128, 32:32 + PAIRS], [[2, PAIRS]], base=2, channel_multiplier=0).then_inc(consts, 1)
            pool.wait_ge(consts, 12)
            g.iota(iota_i[:, 64:64 + NT * TOPK], [[P * TOPK, NT], [1, TOPK]], base=-int(SKIP),
                   channel_multiplier=TOPK).then_inc(consts, 1)
            pool.wait_ge(consts, 13)
            g.tensor_copy(enum[:, :], iota_i[:, 0:E]).then_inc(consts, 1)
            g.tensor_copy(slot_expert[:, :], iota_i[:, 32:32 + PAIRS]).then_inc(consts, 1)
            g.tensor_copy(rows[:, :, H + TOPK:ROW],
                          iota_i[:, 64:64 + NT * TOPK].rearrange("p (i k) -> p i k", i=NT)).then_inc(consts, 1)
            pool.wait_ge(mod01, 1)
            for i in range(NT):
                if i % 4 == 0:
                    continue
                pool.wait_ge(xhat_done, i + 1)
                g.tensor_tensor(h[:, i, :], h[:, i, :], mod[:, 1, :], ALU.mult).then_inc(xhat_scaled, 1)
                if i % 2:
                    pool.wait_ge(xhat_scaled, scaled_by_pool(i))
                    g.tensor_tensor(h[:, i, :], h[:, i, :], mod[:, 0, :], ALU.add).then_inc(h_pool, 1)
            pool.wait_ge(gagb_done, 1)
            pool.wait_ge(h_pool, NB)
            for i in range(NT):
                if i % 2 == 0:
                    pool.wait_ge(h_dve, i // 2 + 1)
                g.tensor_tensor(base[:, i, :], h[:, i, :], mod[:, 2, :], ALU.mult).then_inc(rbase_h, 1)
                pool.wait_ge(rbase_h, i + 1)
                g.tensor_tensor(base[:, i, :], base[:, i, :], xin[:, i, :], ALU.add).then_inc(rbase_done, 1)
            pool.wait_ge(shared_loaded, 48)
            g.tensor_tensor(shd_sb[:, :, :], shd_sb[:, :, :],
                            mod[:, 5, :].unsqueeze(1).to_broadcast([P, FS // P, H]), ALU.mult).then_inc(shd_scaled, 1)
            pool.wait_ge(slots_zeroed, 16)
            for b, (first, count) in enumerate(BATCHES):
                pool.wait_ge(sidx_done, b + 1)
                for i in range(first, first + count):
                    for k in range(TOPK):
                        g.indirect_dma_start(out=slots_d, out_offset=bass.IndirectOffsetOnAxis(
                            ap=slot_idx[:, i, k:k + 1], axis=0), in_=rows[:, i, :], in_offset=None,
                            bounds_check=E * CAP - 1, oob_is_err=False).then_inc(dispatched, 16)
            pool.wait_ge(results_zeroed, 16)
            for r in range(PAIRS):
                if r % 4 == 0:
                    pool.wait_ge(ridx_done, r // 4 + 1)
                if r % 2 == 0:
                    pool.wait_ge(ob_done, r // 2 + 1)
                g.indirect_dma_start(out=results_d, out_offset=bass.IndirectOffsetOnAxis(
                    ap=res_idx[:, r:r + 1], axis=0), in_=ob[:, (r // 2) % 4, (r % 2) * H:(r % 2 + 1) * H],
                    in_offset=None, bounds_check=N * TOPK - 1, oob_is_err=False).then_inc(returned[(r // 2) % 4], 16)

        @block.scalar
        def _(act):
            a = nc.scalar
            a.add_instruction(mybir.InstLoadActFuncSet(
                name=nc.get_next_instruction_name(), engine=a.engine, act_func_set_id=EXP_LN_TABLES, ins=[], outs=[]))
            steps = [0]

            def settle(ins):
                steps[0] += 1
                ins.then_inc(act_step, 1)
                act.wait_ge(act_step, steps[0])

            def rsqrt_seed(n):
                which, first, count = RSQRT[n]
                r = slice(first, first + count)
                act.wait_ge(var_done, n + 1)
                settle(a.activation(lnv[:, which, r], MOMENTS[which][:, r, 1], ACT.Ln, bias=eps[:, 0:1]))
                a.activation(seed[:, which, r], lnv[:, which, r], ACT.Exp, scale=-0.5).then_inc(seed_done, 1)

            act.wait_ge(c_loaded, 16)
            a.activation(cc[:, 1, :], cc[:, 0, :], ACT.Exp, scale=-1.0).then_inc(cexp_done, 1)
            def xhat_tile(i):
                act.wait_ge(xstat_done, i // 4 + 1)
                a.activation(h[:, i, :], xin[:, i, :], ACT.Identity, bias=nmr[:, 0, i:i + 1],
                             scale=rstd[:, 0, i:i + 1]).then_inc(xhat_done, 1)

            def wT_evac(m):
                act.wait_ge(ring_filled, ring[f"wT{m}"] + 1)
                a.copy(wT[:, m], ring_bank(f"wT{m}")[:, :].rearrange("p (j k q) -> p j k q", j=KT, k=KT))\
                 .then_inc(ring_drained, 1)

            def mod_evac(b):
                act.wait_ge(mod_mm, b + 2)
                a.copy(mod[:, 2 + 2 * b:4 + 2 * b, :], MOD_BANK[1 + b][:, :].rearrange("p (m n) -> p m n", m=2))\
                 .then_inc(mod_raw, 1)

            def hn_tile(i):
                act.wait_ge(hstat_done, i // 2 + 1)
                a.activation(hn[:, i, :].rearrange("q (k p) -> q p k", k=KT),
                             h[:, i, :].rearrange("q (p k) -> q p k", k=KT), ACT.Identity,
                             bias=nmr[:, 1, i:i + 1], scale=rstd[:, 1, i:i + 1]).then_inc(hn_done, 1)

            def xn_evac(j):
                act.wait_ge(ring_filled, ring[f"hn{j}"] + 1)
                for k in range(KT):
                    last = a.activation(xnT[:, k, 256 * j:256 * j + 256],
                                        ring_bank(f"hn{j}")[:, 256 * k:256 * k + 256], ACT.Identity,
                                        bias=gb_col[:, 1, k:k + 1], scale=gb_col[:, 0, k:k + 1])
                last.then_inc(ring_drained, 1)

            def q_evac(half):
                act.wait_ge(qT_mm, half + 1)
                a.copy(qT[:, 0, 512 * half:512 * half + 512], bank[1][:, :]).then_inc(qT_act, 1)

            def exp_tile(i):
                act.wait_ge(nmax_done, i + 1)
                n = P * (i + 1)
                if i == 0:
                    act.wait_ge(slots_zeroed, 16)
                    act.wait_ge(results_zeroed, 16)
                for b in range((n + 511) // 512):
                    w = min(512, n - 512 * b)
                    last = a.activation(prob[:, i % 2, 512 * b:512 * b + w], bank[2 * (i % 2) + b][:, 0:w], ACT.Exp,
                                        bias=nmax[:, i:i + 1], scale=SCALE, accum_out=esum[:, i, b:b + 1])
                last.then_inc(exp_done, 1)

            def p_evac(i):
                for g in range(i // 4 + 1):
                    act.wait_ge(ring_filled, ring[f"p{i}.{g}"] + 1)
                    if i >= 2:
                        act.wait_ge(pv_mm, i - 1)
                    w = min(4, i + 1 - 4 * g)
                    a.copy(probT[:, i % 2, 4 * g:4 * g + w, :],
                           ring_bank(f"p{i}.{g}")[:, 0:P * w].rearrange("p (j q) -> p j q", j=w))\
                     .then_inc(ring_drained, 1)

            def h2_evac(i):
                act.wait_ge(ring_filled, ring[f"x{i}"] + 1)
                if i == 0:
                    act.wait_ge(modc_done, 1)
                for k in range(KT):
                    last = a.activation(h2T[:, k, P * i:P * i + P], ring_bank(f"x{i}")[:, P * k:P * k + P],
                                        ACT.Identity, bias=modc[:, 1, k:k + 1], scale=modc[:, 0, k:k + 1])
                last.then_inc(ring_drained, 1)

            def gate_exp(b):
                act.wait_ge(logits_mm, b + 1)
                if b >= 1:
                    act.wait_ge(score_done, b)
                n = BATCHES[b][1]
                a.activation(r_ex[:, 0:n, :], bank[7][:, 0:n * E].rearrange("p (t e) -> p t e", t=n), ACT.Exp,
                             scale=-1.0).then_inc(gexp_done, 1)

            act.wait_ge(consts, 2)
            rsqrt_seed(0)
            for i in range(4):
                xhat_tile(i)
            rsqrt_seed(1)
            wT_evac(0)
            for i in range(4, NT):
                xhat_tile(i)
            wT_evac(1)
            wT_evac(2)
            rsqrt_seed(2)
            act.wait_ge(wqk_mm, 1)
            a.copy(wqk, bank[3][:, :].rearrange("p (k n) -> p k n", k=KT)).then_inc(wqk_done, 1)
            rsqrt_seed(3)
            for i in range(4):
                hn_tile(i)
            act.wait_ge(small_loaded, 64)
            xn_evac(0)
            xn_evac(1)
            rsqrt_seed(4)
            rsqrt_seed(5)
            mod_evac(0)
            mod_evac(1)
            q_evac(0)
            act.wait_ge(ring_filled, ring["gateT"] + 1)
            a.copy(gateT[:, :, :], ring_bank("gateT")[:, 0:KT * E].rearrange("p (k e) -> p k e", k=KT))\
             .then_inc(ring_drained, 1)
            for i in range(4, NT):
                hn_tile(i)
            xn_evac(2)
            exp_tile(0)
            xn_evac(3)
            exp_tile(1)
            for i in range(NT):
                p_evac(i)
                if i in (4, 6):
                    gate_exp(i // 2 - 2)
                if i + 2 < NT:
                    exp_tile(i + 2)
                if i == 1:
                    rsqrt_seed(6 + i)
                    q_evac(1)
                if i >= 1:
                    h2_evac(i - 1)
                if i == NT - 1:
                    gate_exp(2)
                if i != 1:
                    rsqrt_seed(6 + i)
            h2_evac(NT - 1)
            gate_exp(3)
            for half in range(2):
                for ft in range(FS // P):
                    act.wait_ge(sh_mm, SH_COUNT[half, 0, ft])
                    a.activation(sh_act[:, ft + 2 * half, :], SH_BANK[half, 0, ft][:, :], ACT.Silu)\
                     .then_inc(sh_silu, 1)
            def slot_evac(c):
                act.wait_ge(slotT_mm, c + 1)
                a.activation(slotT[:, 0, 512 * c:512 * c + 512], bank[0][:, :], ACT.Identity,
                             bias=modc[:, 1, 0:1], scale=modc[:, 0, 0:1]).then_inc(slotT_act, 1)

            def hid_evac(g):
                act.wait_ge(hidT_mm, g + 1)
                if g >= 2:
                    act.wait_ge(down_mm, g - 1)
                a.copy(hidT[:, g % 2], bank[2 + g % 2][:, 0:256].rearrange("p (r s) -> p r s", r=2))\
                 .then_inc(hidT_done, 1)

            act.wait_ge(weights_done, 1)
            act.wait_ge(shd_mm, NB)
            slot_evac(0)
            for g in range(EGROUPS):
                if g % 2 == 0 and g // 2 + 1 < CHUNKS:
                    slot_evac(g // 2 + 1)
                if g >= 1:
                    hid_evac(g - 1)
                act.wait_ge(up_mm, g + 1)
                if g >= 2:
                    act.wait_ge(hid_done, g - 1)
                a.activation(act_h[:, g % 2], bank[4 + g % 2][:, :].rearrange("p (r w f) -> p r w f", r=2, w=2)[:, :, 0, :],
                             ACT.Silu).then_inc(silu_done, 1)
                for k in range(3):
                    last = a.activation(diag[3 * g + k], ident[:, :], ACT.Copy, scale=wk[:, g, k:k + 1])
                last.then_inc(diag_done, 1)
            hid_evac(EGROUPS - 1)

        @block.vector
        def _(dve):
            v = nc.vector
            steps = [0]

            def step(ins):
                steps[0] += 1
                ins.then_inc(dve_step, 1)

            def settle():
                dve.wait_ge(dve_step, steps[0])

            def chain(ins):
                step(ins)
                settle()

            dve.wait_ge(cexp_done, 1)
            chain(v.tensor_scalar(cc[:, 2, :], cc[:, 1, :], 1.0, None, ALU.add))
            chain(v.reciprocal(cc[:, 3, :], cc[:, 2, :]))
            chain(v.tensor_tensor(cc[:, 1, :], cc[:, 0, :], cc[:, 3, :], ALU.mult))
            v.tensor_copy(silu_c[:, :, :], cc[:, 1, :].unsqueeze(2).to_broadcast([P, KT, P])).then_inc(silu_c_done, 1)

            def moments(n, src):
                which, first, count = RSQRT[n]
                tiles, mv = range(first, first + count), MOMENTS[which]
                for i in tiles:
                    step(v.bn_stats(st[:, i, :], src[:, i, :]))
                settle()
                for i in tiles:
                    last = v.bn_aggr(mv[:, i, :], st[:, i, :])
                last.then_inc(var_done, 1)
                dve.wait_ge(var_done, n + 1)
                r = slice(first, first + count)
                step(v.tensor_scalar(half_v[:, which, r], mv[:, r, 1], LN_EPS, -0.5, ALU.add, ALU.mult))

            def refine(n):
                which, first, count = RSQRT[n]
                r = slice(first, first + count)
                dve.wait_ge(seed_done, n + 1)
                settle()
                chain(v.tensor_tensor(newt[:, which, r], half_v[:, which, r], seed[:, which, r], ALU.mult))
                chain(v.tensor_tensor(newt[:, which, r], newt[:, which, r], seed[:, which, r], ALU.mult))
                chain(v.scalar_tensor_tensor(out=rstd[:, which, r], in0=newt[:, which, r], scalar=1.5,
                                             in1=seed[:, which, r], op0=ALU.add, op1=ALU.mult))

            def x_moments(n):
                for j in (2 * n, 2 * n + 1):
                    dve.wait_ge(x_loaded[j], 16)
                moments(n, xin)

            def shift(n, done):
                which, first, count = RSQRT[n]
                refine(n)
                r = slice(first, first + count)
                v.scalar_tensor_tensor(out=nmr[:, which, r], in0=MOMENTS[which][:, r, 0], scalar=-1.0,
                                       in1=rstd[:, which, r], op0=ALU.mult, op1=ALU.mult).then_inc(done, 1)

            def make_h(j):
                if j % 2 == 0:
                    dve.wait_ge(xhat_done, 2 * j + 1)
                    chain(v.tensor_tensor(h[:, 2 * j, :], h[:, 2 * j, :], mod[:, 1, :], ALU.mult))
                else:
                    dve.wait_ge(xhat_scaled, scaled_by_pool(2 * j))
                v.tensor_tensor(h[:, 2 * j, :], h[:, 2 * j, :], mod[:, 0, :], ALU.add).then_inc(h_dve, 1)
                dve.wait_ge(h_dve, j + 1)
                dve.wait_ge(h_pool, j + 1)
                moments(2 + j, h)

            def mod01_evac():
                dve.wait_ge(mod_mm, 1)
                v.tensor_copy(mod[:, 0, :], bank[0][:, 0:H])
                v.tensor_scalar(mod[:, 1, :], bank[0][:, H:2 * H], 1.0, None, ALU.add).then_inc(mod01, 1)
                dve.wait_ge(mod01, 1)

            def gates():
                dve.wait_ge(mod_raw, 2)
                both = mod[:, 2:6:3, :]
                chain(v.scalar_tensor_tensor(out=gabs[:, :, :], in0=both, scalar=-1.0, in1=both,
                                             op0=ALU.mult, op1=ALU.max))
                step(v.tensor_scalar(gabs[:, :, :], gabs[:, :, :], 0.25, None, ALU.max))
                chain(v.tensor_scalar(both, both, 0.0, 2.0, ALU.is_ge, ALU.mult))
                v.scalar_tensor_tensor(out=both, in0=both, scalar=1.0, in1=gabs[:, :, :],
                                       op0=ALU.subtract, op1=ALU.mult).then_inc(gagb_done, 1)
                dve.wait_ge(gagb_done, 1)

            def mod_columns():
                dve.wait_ge(modc_mm, 1)
                v.tensor_copy(modc[:, 1, :], bank[7][:, 0:KT])
                v.tensor_scalar(modc[:, 0, :], bank[7][:, KT:2 * KT], 1.0, None, ALU.add).then_inc(modc_done, 1)

            def wvo_evac():
                dve.wait_ge(wvo_mm, 1)
                v.tensor_tensor(wvo, bank[6][:, :].rearrange("p (k n) -> p k n", k=KT),
                                mod[:, 2, :].unsqueeze(1).to_broadcast([P, KT, H]), ALU.mult).then_inc(wvo_done, 1)

            def q_evac(half):
                dve.wait_ge(qT_mm, half + 1)
                v.tensor_copy(qT[:, 1, 512 * half:512 * half + 512], bank[3][:, :]).then_inc(qT_dve, 1)

            def vo_evac(j):
                dve.wait_ge(vo_mm, j + 1)
                v.tensor_copy(vo[:, 2 * j:2 * j + 2, :],
                              bank[6 + j % 2][:, :].rearrange("p (i n) -> p i n", i=2)).then_inc(vo_done, 1)

            def row_max(i):
                dve.wait_ge(scores_mm, i + 1)
                n = P * (i + 1)
                nb = (n + 511) // 512
                for b in range(nb):
                    w = min(512, n - 512 * b)
                    step(v.tensor_reduce(bmax[:, i, b:b + 1], bank[2 * (i % 2) + b][:, 0:w], AX_X, ALU.max))
                settle()
                if nb == 2:
                    chain(v.tensor_tensor(bmax[:, i, 0:1], bmax[:, i, 0:1], bmax[:, i, 1:2], ALU.max))
                v.tensor_scalar(nmax[:, i:i + 1], bmax[:, i, 0:1], -SCALE, None, ALU.mult).then_inc(nmax_done, 1)

            def add_attention(i):
                dve.wait_ge(exp_done, i + 1)
                if i >= 4:
                    chain(v.tensor_tensor(esum[:, i, 0:1], esum[:, i, 0:1], esum[:, i, 1:2], ALU.add))
                chain(v.reciprocal(rinv[:, i:i + 1], esum[:, i, 0:1]))
                dve.wait_ge(rbase_done, i + 1)
                dve.wait_ge(pv_mm, i + 1)
                v.scalar_tensor_tensor(out=base[:, i, :], in0=bank[6][:, 0:H], scalar=rinv[:, i:i + 1],
                                       in1=base[:, i, :], op0=ALU.mult, op1=ALU.add).then_inc(x2_done, 1)
                dve.wait_ge(x2_done, i + 1)
                moments(6 + i, base)

            def norm_x2(i):
                refine(6 + i)
                v.tensor_scalar(rows[:, i, 0:H].rearrange("q (k p) -> q p k", k=KT),
                                base[:, i, :].rearrange("q (p k) -> q p k", k=KT), mv3[:, i, 0:1],
                                rstd[:, 2, i:i + 1], ALU.subtract, ALU.mult).then_inc(rows_done, 1)

            def route_scores(b):
                first, n = BATCHES[b]
                four = [P, n, GROUPS, GROUPS]
                sc, out_s = r_sc[:, 0:n, :], score[:, first:first + n, :]
                dve.wait_ge(gexp_done, b + 1)
                chain(v.tensor_scalar(sc, r_ex[:, 0:n, :], 1.0, None, ALU.add))
                v.reciprocal(out_s, sc).then_inc(score_done, 1)
                dve.wait_ge(score_done, b + 1)
                chain(v.tensor_tensor(sc, out_s, bias_b[:, :].unsqueeze(1).to_broadcast([P, n, E]), ALU.add))
                s = sc.rearrange("p t (g e) -> p t g e", g=GROUPS)
                for i in range(n):
                    for g in range(GROUPS):
                        step(v.max(g_top[:, i, g, :], s[:, i, g, :]))
                settle()
                total = g_sum[:, 0:n]
                chain(v.tensor_tensor(total, g_top[:, 0:n, :, 0], g_top[:, 0:n, :, 1], ALU.add))
                other, own = total.unsqueeze(2).to_broadcast(four), total.unsqueeze(3).to_broadcast(four)
                gt, eq = g_cmp[:, 0:n, :, 0:GROUPS], g_cmp[:, 0:n, :, GROUPS:]
                step(v.tensor_tensor(gt, other, own, ALU.is_gt))
                chain(v.tensor_tensor(eq, other, own, ALU.is_equal))
                chain(v.tensor_tensor(eq, eq, lower[:, :, :].unsqueeze(1).to_broadcast(four), ALU.mult))
                step(v.tensor_reduce(g_rank[:, 0:n], g_cmp[:, 0:n], AX_X, ALU.add))

            def route_choose(b):
                first, n = BATCHES[b]
                settle()
                chain(v.scalar_tensor_tensor(
                    out=chosen[:, 0:n, :].rearrange("p t (g e) -> p t g e", g=GROUPS),
                    in0=g_rank[:, 0:n, :].unsqueeze(3).to_broadcast([P, n, GROUPS, EG]), scalar=float(TOP_GROUPS),
                    in1=r_sc[:, 0:n, :].rearrange("p t (g e) -> p t g e", g=GROUPS), op0=ALU.is_lt, op1=ALU.mult))
                for t in range(n):
                    step(v.max(top8[:, t, :], chosen[:, t, :]))
                settle()
                for t in range(n):
                    step(v.max_index(idx8[:, t, :], top8[:, t, :], chosen[:, t, :]))
                settle()
                names = rows[:, first:first + n, H:H + TOPK]
                chain(v.tensor_scalar(names, idx8[:, 0:n, 0:TOPK], 1.0, None, ALU.add))
                shape = [P, n, TOPK, E]
                mine = hot[:, first:first + n]
                chain(v.tensor_tensor(mine, enum[:, :].unsqueeze(1).unsqueeze(1).to_broadcast(shape),
                                      names.unsqueeze(3).to_broadcast(shape), ALU.is_equal))
                with nc.allow_low_precision("0 or 1"):
                    v.tensor_reduce(mask_bf[:, first:first + n, :], mine.rearrange("p t k e -> p t e k"),
                                    AX_X, ALU.add).then_inc(mask_done, 1)

            def route_weights():
                dve.wait_ge(sidx_done, len(BATCHES))
                chain(v.tensor_tensor(hot, hot, score.unsqueeze(2).to_broadcast([P, NT, TOPK, E]), ALU.mult))
                chain(v.tensor_reduce(sk[:, :, :], hot, AX_X, ALU.add))
                chain(v.tensor_reduce(ssum[:, :, 0], sk[:, :, :], AX_X, ALU.add))
                chain(v.tensor_scalar(ssum[:, :, 0], ssum[:, :, 0], 1e-20, None, ALU.add))
                chain(v.reciprocal(ssum[:, :, 1], ssum[:, :, 0]))
                v.scalar_tensor_tensor(out=wk[:, :, :], in0=sk[:, :, :], scalar=ROUTED_SCALE,
                                       in1=ssum[:, :, 1].unsqueeze(2).to_broadcast([P, NT, TOPK]),
                                       op0=ALU.mult, op1=ALU.mult).then_inc(weights_done, 1)

            def route_place(b):
                first, n = BATCHES[b]
                dve.wait_ge(pos_mm, b + 1)
                settle()
                v.tensor_tensor(hotx[:, 0:n], hot[:, first:first + n],
                                bank[7][:, POS:POS + n * E].rearrange("p (t e) -> p t e", t=n).unsqueeze(2)
                                .to_broadcast([P, n, TOPK, E]), ALU.mult).then_inc(pos_read, 1)
                dve.wait_ge(pos_read, b + 1)
                chain(v.tensor_reduce(pk[:, 0:n, :], hotx[:, 0:n], AX_X, ALU.add))
                step(v.tensor_scalar(pbig[:, 0:n, :], pk[:, 0:n, :], float(CAP), SKIP, ALU.is_ge, ALU.mult))
                chain(v.scalar_tensor_tensor(out=pidx[:, 0:n, :], in0=rows[:, first:first + n, H:H + TOPK],
                                             scalar=float(CAP), in1=pk[:, 0:n, :], op0=ALU.mult, op1=ALU.add))
                v.scalar_tensor_tensor(out=slot_idx[:, first:first + n, :], in0=pidx[:, 0:n, :], scalar=-float(CAP),
                                       in1=pbig[:, 0:n, :], op0=ALU.add, op1=ALU.add).then_inc(sidx_done, 1)

            x_moments(0)
            shift(0, xstat_done)
            x_moments(1)
            mod01_evac()
            shift(1, xstat_done)
            make_h(0)
            make_h(1)
            shift(2, hstat_done)
            shift(3, hstat_done)
            make_h(2)
            make_h(3)
            shift(4, hstat_done)
            shift(5, hstat_done)
            gates()
            q_evac(0)
            wvo_evac()
            row_max(0)
            row_max(1)
            mod_columns()
            for j in range(2):
                vo_evac(j)
            dve.wait_ge(consts, 16)
            dve.wait_ge(small_loaded, 64)
            for i in range(NT):
                if i < 2:
                    vo_evac(2 + i)
                if i == 4:
                    dve.wait_ge(rbase_done, NT)
                if i in (4, 6):
                    route_scores(i // 2 - 2)
                if i + 2 < NT:
                    row_max(i + 2)
                if i == 5:
                    route_place(0)
                if i == NT - 1:
                    route_place(1)
                    route_scores(2)
                add_attention(i)
                if i == 1:
                    q_evac(1)
                norm_x2(i)
                if i in (4, 6):
                    route_choose(i // 2 - 2)
            route_choose(2)
            route_place(2)
            route_scores(3)
            route_choose(3)
            route_place(3)
            for half in range(2):
                for ft in range(FS // P):
                    dve.wait_ge(sh_silu, 2 * half + ft + 1)
                    dve.wait_ge(sh_mm, SH_COUNT[half, 1, ft])
                    v.tensor_tensor(aT[:, ft, 512 * half:512 * half + 512], sh_act[:, ft + 2 * half, :],
                                    SH_BANK[half, 1, ft][:, :], ALU.mult).then_inc(sh_hid, 1)
            route_weights()
            for j in range(NB):
                dve.wait_ge(shd_mm, j + 1)
                v.tensor_tensor(base[:, 2 * j:2 * j + 2, :], SHD_BANK[j][:, :].rearrange("p (i n) -> p i n", i=2),
                                base[:, 2 * j:2 * j + 2, :], ALU.add).then_inc(base_done, 1)

            def slot_meta(g):
                dve.wait_ge(slots_loaded[g], 16)
                r = slice(4 * g, 4 * g + 4)
                chain(v.tensor_tensor(m_eq[:, :, :], slot_in[:, r, H:H + TOPK],
                                      slot_expert[:, r].unsqueeze(2).to_broadcast([P, 4, TOPK]), ALU.is_equal))
                chain(v.tensor_tensor(m_eq[:, :, :], m_eq[:, :, :], slot_in[:, r, H + TOPK:ROW], ALU.mult))
                chain(v.tensor_reduce(m_row[:, :], m_eq[:, :, :], AX_X, ALU.add))
                v.tensor_scalar(res_idx[:, r], m_row[:, :], SKIP, None, ALU.add).then_inc(ridx_done, 1)

            def slot_evac(c):
                dve.wait_ge(slotT_mm, c + 1)
                v.tensor_scalar(slotT[:, 1, 512 * c:512 * c + 512], bank[1][:, :],
                                modc[:, 0, 1:2], modc[:, 1, 1:2], ALU.mult, ALU.add).then_inc(slotT_dve, 1)

            def expert_evac(g):
                dve.wait_ge(down_mm, g + 1)
                if g >= 4:
                    dve.wait_ge(returned[g % 4], 16 * 2 * (g // 4))
                v.tensor_tensor(ob[:, g % 4, :].rearrange("p (r n) -> p r n", r=2),
                                bank[6 + g % 2][:, :].rearrange("p (r n) -> p r n", r=2),
                                mod[:, 5, :].unsqueeze(1).to_broadcast([P, 2, H]), ALU.mult).then_inc(ob_done, 1)

            slot_evac(0)
            slot_meta(0)
            for g in range(EGROUPS):
                if g % 2 == 0 and g // 2 + 1 < CHUNKS:
                    slot_evac(g // 2 + 1)
                    slot_meta(g // 2 + 1)
                dve.wait_ge(silu_done, g + 1)
                if g >= 2:
                    dve.wait_ge(hidT_mm, g - 1)
                v.tensor_tensor(hid[:, g % 2], act_h[:, g % 2],
                                bank[4 + g % 2][:, :].rearrange("p (r w f) -> p r w f", r=2, w=2)[:, :, 1, :],
                                ALU.mult).then_inc(hid_done, 1)
                if g >= 1:
                    expert_evac(g - 1)
            expert_evac(EGROUPS - 1)
            for i in range(NT):
                dve.wait_ge(y_loaded[i], 16)
                chain(v.scalar_tensor_tensor(out=base[:, i, :], in0=yin[i][:, H * 3:H * 4],
                                             scalar=wk[:, i, 3:4], in1=base[:, i, :], op0=ALU.mult, op1=ALU.add))
                dve.wait_ge(sum_mm, i + 1)
                v.tensor_tensor(base[:, i, :], base[:, i, :], bank[i % 4][:, 0:H], ALU.add).then_inc(final_done, 1)

        @block.tensor
        def _(pe):
            t = nc.tensor

            def ring_open(name):
                n = ring[name]
                if n >= 2:
                    pe.wait_ge(ring_drained, n - 1)
                return ring_bank(name)

            def product(dst, terms):
                for n, (lhsT, rhs) in enumerate(terms):
                    last = t.matmul(dst, lhsT, rhs, start=(n == 0), stop=(n == len(terms) - 1))
                return last

            def mod_rows(b):
                w = wmod_b[:, :, 512 * b - 512:512 * b] if b else wmod_a
                product(MOD_BANK[b][:, :], [(silu_c[:, k, :], w[:, k, :]) for k in range(KT)])\
                    .then_inc(mod_mm, 1)

            pe.wait_ge(silu_c_done, 1)
            pe.wait_ge(wmod_loaded[0], 16)
            mod_rows(0)
            pe.wait_ge(consts, 3)
            pe.wait_ge(qkv_loaded, 16)
            for m in range(3):
                b = ring_open(f"wT{m}")
                for j in range(KT):
                    for k in range(KT):
                        o = P * (KT * j + k)
                        last = t.transpose(b[:, o:o + P], qkv_sb[:, k, H * m + P * j:H * m + P * j + P], ident[:, :])
                last.then_inc(ring_filled, 1)
            def fold_qk():
                pe.wait_ge(ring_drained, ring["wT1"] + 1)
                for k in range(KT):
                    last = product(bank[3][:, H * k:H * k + H],
                                   [(wT[:, 0, j, k, :], wT[:, 1, j].rearrange("p k q -> p (k q)")) for j in range(KT)])
                last.then_inc(wqk_mm, 1)

            def fold_vo():
                pe.wait_ge(ring_drained, ring["wT2"] + 1)
                pe.wait_ge(wo_loaded, 16)
                for k in range(KT):
                    last = product(bank[6][:, H * k:H * k + H], [(wT[:, 2, j, k, :], wo_sb[:, j, :])
                                                                 for j in range(KT)])
                last.then_inc(wvo_mm, 1)

            def turn_gate():
                pe.wait_ge(small_loaded, 64)
                b = ring_open("gateT")
                for k in range(KT):
                    last = t.transpose(b[:, E * k:E * k + E], gatew_sb[:, k::KT], ident[0:E, 0:E])
                last.then_inc(ring_filled, 1)

            def mod_by_partition():
                pe.wait_ge(mod_raw, 2)
                for n, m in enumerate((3, 4)):
                    for k in range(KT):
                        last = t.matmul(bank[7][:, KT * n + k:KT * n + k + 1], mod[0:1, m, k::KT], ones_f[0:1, 0:1],
                                        start=True, stop=True)
                last.then_inc(modc_mm, 1)

            def turn_h(j):
                pe.wait_ge(hn_done, 2 * j + 2)
                b = ring_open(f"hn{j}")
                for i in range(2):
                    for k in range(KT):
                        last = t.transpose(b[:, 256 * k + P * i:256 * k + P * i + P], hn[:, 2 * j + i, P * k:P * k + P],
                                           ident[:, :])
                last.then_inc(ring_filled, 1)

            def project_q(half):
                pe.wait_ge(ring_drained, ring[f"hn{2 * half + 1}"] + 1)
                pe.wait_ge(wqk_done, 1)
                if half:
                    pe.wait_ge(qT_act, 1)
                    pe.wait_ge(qT_dve, 1)
                for d in range(KT):
                    last = product(bank[1 + 2 * d][:, :], [(wqk[:, k, P * d:P * d + P],
                                                            xnT[:, k, 512 * half:512 * half + 512]) for k in range(KT)])
                last.then_inc(qT_mm, 1)

            def project_v(j):
                pe.wait_ge(ring_drained, ring[f"hn{j}"] + 1)
                pe.wait_ge(wvo_done, 1)
                pe.wait_ge(modc_done, 1)
                if j >= 2:
                    pe.wait_ge(vo_done, j - 1)
                for i in range(2):
                    tok = slice(256 * j + P * i, 256 * j + P * i + P)
                    last = product(bank[6 + j % 2][:, H * i:H * i + H], [(xnT[:, k, tok], wvo[:, k, :])
                                                                         for k in range(KT)])
                last.then_inc(vo_mm, 1)

            def scores(i):
                if i % 4 == 0:
                    pe.wait_ge(qT_act, i // 4 + 1)
                    pe.wait_ge(qT_dve, i // 4 + 1)
                if i >= 2:
                    pe.wait_ge(exp_done, i - 1)
                else:
                    pe.wait_ge(mod01, 1)
                    pe.wait_ge(mod_raw, 1)
                    pe.wait_ge(consts, 8)
                n = P * (i + 1)
                for b in range((n + 511) // 512):
                    w = min(512, n - 512 * b)
                    dst = bank[2 * (i % 2) + b]
                    t.matmul(dst[:, 0:w], qT[:, 0, P * i:P * i + P], xnT[:, 0, 512 * b:512 * b + w],
                             start=True, stop=False)
                    if b == i // 4:
                        t.matmul(dst[:, w - P:w], ident_bf[:, :], causal_bf[:, :], start=False, stop=False)
                    last = t.matmul(dst[:, 0:w], qT[:, 1, P * i:P * i + P], xnT[:, 1, 512 * b:512 * b + w],
                                    start=False, stop=True)
                last.then_inc(scores_mm, 1)

            def turn_p(i):
                pe.wait_ge(exp_done, i + 1)
                for g in range(i // 4 + 1):
                    b = ring_open(f"p{i}.{g}")
                    for j in range(4 * g, min(4 * g + 4, i + 1)):
                        last = t.transpose(b[:, P * (j - 4 * g):P * (j - 4 * g) + P], prob[:, i % 2, P * j:P * j + P],
                                           ident[:, :])
                    last.then_inc(ring_filled, 1)

            def weigh_v(i):
                pe.wait_ge(vo_done, max(i // 2 + 1, 3))
                if i >= 1:
                    pe.wait_ge(x2_done, i)
                for j in range(i + 1):
                    if j % 4 == 0:
                        pe.wait_ge(ring_drained, ring[f"p{i}.{j // 4}"] + 1)
                    last = t.matmul(bank[6][:, 0:H], probT[:, i % 2, j, :], vo[:, j, :], start=(j == 0), stop=(j == i))
                last.then_inc(pv_mm, 1)

            def turn_x(i):
                pe.wait_ge(rows_done, i + 1)
                b = ring_open(f"x{i}")
                for k in range(KT):
                    last = t.transpose(b[:, P * k:P * k + P], rows[:, i, P * k:P * k + P], ident[:, :])
                last.then_inc(ring_filled, 1)

            def logits(b):
                first, n = BATCHES[b]
                pe.wait_ge(ring_drained, ring[f"x{first + n - 1}"] + 1)
                if b >= 1:
                    pe.wait_ge(gexp_done, b)
                    pe.wait_ge(pos_read, (0, 1, 1, 2)[b])
                else:
                    pe.wait_ge(vo_done, NB)
                for i in range(n):
                    tok = slice(P * (first + i), P * (first + i) + P)
                    last = product(bank[7][:, E * i:E * i + E], [(h2T[:, k, tok], gateT[:, k, :]) for k in range(KT)])
                last.then_inc(logits_mm, 1)

            def positions(b):
                first, n = BATCHES[b]
                pe.wait_ge(mask_done, b + 1)
                pe.wait_ge(gexp_done, (1, 3, 4, 4)[b])
                if b >= 2:
                    pe.wait_ge(pos_read, b)
                for i in range(first, first + n):
                    o = POS + E * (i - first)
                    last = product(bank[7][:, o:o + E], [(earlier_bf[:, :], mask_bf[:, i, :])]
                                   + [(ones_bf[:, :], mask_bf[:, j, :]) for j in range(i)])
                last.then_inc(pos_mm, 1)

            def shared_up_part(key):
                half, what, ft = key
                w = (shg_sb, shu_sb)[what]
                product(SH_BANK[key][:, :], [(w[:, k, P * ft:P * ft + P], h2T[:, k, 512 * half:512 * half + 512])
                                             for k in range(KT)]).then_inc(sh_mm, 1)

            pe.wait_ge(wmod_loaded[1], 16)
            mod_rows(1)
            fold_qk()
            fold_vo()
            turn_h(0)
            mod_rows(2)
            turn_h(1)
            project_q(0)
            turn_gate()
            turn_h(2)
            scores(0)
            scores(1)
            mod_by_partition()
            turn_h(3)
            project_v(0)
            project_v(1)
            for i in range(NT):
                turn_p(i)
                if i in (4, 6):
                    logits(i // 2 - 2)
                if i < 2:
                    project_v(2 + i)
                if i + 2 < NT:
                    scores(i + 2)
                if i == 5:
                    positions(0)
                if i == NT - 1:
                    turn_x(i - 1)
                    pe.wait_ge(shared_loaded, 48)
                    shared_up_part(SH_ORDER[0])
                    logits(2)
                    positions(1)
                weigh_v(i)
                if i == 1:
                    project_q(1)
                if 1 <= i < NT - 1:
                    turn_x(i - 1)
            shared_up_part(SH_ORDER[1])
            turn_x(NT - 1)
            shared_up_part(SH_ORDER[2])
            logits(3)
            positions(2)
            shared_up_part(SH_ORDER[3])
            pe.wait_ge(x2_done, NT)
            shared_up_part(SH_ORDER[4])
            pe.wait_ge(ring_drained, ring[f"x{NT - 1}"] + 1)
            shared_up_part(SH_ORDER[5])
            positions(3)
            shared_up_part(SH_ORDER[6])
            pe.wait_ge(sh_silu, 1)
            shared_up_part(SH_ORDER[7])
            pe.wait_ge(shd_scaled, 1)
            for j in range(NB):
                pe.wait_ge(sh_hid, (2, 2, 4, 4)[j])
                if j < 3:
                    pe.wait_ge(sh_silu, 2)
                for i in range(2):
                    tok = slice(P * (2 * j + i), P * (2 * j + i) + P)
                    last = product(SHD_BANK[j][:, H * i:H * i + H], [(aT[:, f, tok], shd_sb[:, f, :])
                                                                     for f in range(FS // P)])
                last.then_inc(shd_mm, 1)

            def turn_slots(c):
                pe.wait_ge(slots_loaded[c], 16)
                if c >= 1:
                    pe.wait_ge(slotT_act, c)
                    pe.wait_ge(slotT_dve, c)
                else:
                    pe.wait_ge(base_done, NB)
                    pe.wait_ge(sh_hid, 4)
                for k in range(KT):
                    for r in range(4):
                        last = t.transpose(bank[k][:, P * r:P * r + P],
                                           slot_in[:, 4 * c + r, P * k:P * k + P], ident[:, :])
                last.then_inc(slotT_mm, 1)

            def expert_up(g):
                if g % 2 == 0:
                    pe.wait_ge(experts_loaded[g // 2], 48)
                    pe.wait_ge(slotT_act, g // 2 + 1)
                    pe.wait_ge(slotT_dve, g // 2 + 1)
                if g >= 2:
                    pe.wait_ge(hid_done, g - 1)
                for r in range(2):
                    for what, w in enumerate((w1_sb, w3_sb)):
                        if g >= 1 and (r, what) == (1, 1):
                            turn_hid(g - 1)
                        o = 256 * r + P * what
                        for k in range(KT):
                            for side in range(2):
                                e = 4 * g + 2 * r + side
                                last = t.matmul(bank[4 + g % 2][CAP * side:CAP * side + CAP, o:o + F],
                                                slotT[:, k, CAP * e:CAP * e + CAP], w[:, e, k, :],
                                                start=(k == 0), stop=(k == KT - 1))
                last.then_inc(up_mm, 1)

            def turn_hid(g):
                pe.wait_ge(hid_done, g + 1)
                if g >= 2:
                    pe.wait_ge(hidT_done, g - 1)
                for r in range(2):
                    last = t.transpose(bank[2 + g % 2][:, P * r:P * r + P], hid[:, g % 2, r, :], ident[:, :])
                last.then_inc(hidT_mm, 1)

            def expert_down(g):
                pe.wait_ge(hidT_done, g + 1)
                if g >= 2:
                    pe.wait_ge(ob_done, g - 1)
                for r in range(2):
                    for side in range(2):
                        last = t.matmul(bank[6 + g % 2][CAP * side:CAP * side + CAP, H * r:H * r + H],
                                        hidT[:, g % 2, r, CAP * side:CAP * side + CAP],
                                        w2_sb[:, 4 * g + 2 * r + side, :], start=True, stop=True)
                last.then_inc(down_mm, 1)

            turn_slots(0)
            for g in range(EGROUPS):
                if g % 2 == 0 and g // 2 + 1 < CHUNKS:
                    turn_slots(g // 2 + 1)
                expert_up(g)
                if g >= 1:
                    expert_down(g - 1)
            turn_hid(EGROUPS - 1)
            expert_down(EGROUPS - 1)
            for i in range(NT):
                pe.wait_ge(y_loaded[i], 16)
                pe.wait_ge(diag_done, i + 1)
                if i >= 4:
                    pe.wait_ge(final_done, i - 3)
                else:
                    pe.wait_ge(hidT_done, EGROUPS)
                    pe.wait_ge(slotT_dve, CHUNKS)
                product(bank[i % 4][:, 0:H], [(diag[3 * i + k], yin[i][:, H * k:H * k + H]) for k in range(3)])\
                    .then_inc(sum_mm, 1)


_INS = ['L0_attn_x', 'L0_attn_qkv', 'L0_attn_o_proj', 'L0_attn_gamma', 'L0_attn_beta', 'L0_ffn_gate_w',
        'L0_ffn_gate_bias', 'L0_ffn_w1', 'L0_ffn_w2', 'L0_ffn_w3', 'L0_ffn_shared_gate', 'L0_ffn_shared_up',
        'L0_ffn_shared_down', 'L0_c', 'L0_wmod']


def kernel(**inputs):
    import numpy as _np
    import concourse.bacc as _bacc
    from concourse import mybir as _mybir
    from concourse.bass_utils import run_bass_kernel_spmd as _run

    nc = _bacc.Bacc("TRN2", target_bir_lowering=False, num_devices=1)
    arrays, args = {}, []
    for name in _INS:
        a = _np.ascontiguousarray(inputs[name])
        arrays[f"in_{name}_dram"] = a
        args.append(nc.dram_tensor(f"in_{name}_dram", a.shape, _mybir.dt.from_np(a.dtype), kind="ExternalInput").ap())
    shape = inputs['L0_attn_x'].shape
    args.append(nc.dram_tensor("out_0_dram", shape, _mybir.dt.from_np(_np.dtype("float32")),
                               kind="ExternalOutput").ap())
    adaln_attention_moe(nc, *args)
    r = _run(nc, [arrays], core_ids=[0])
    return r.results[0]["out_0_dram"]
```
